# Optimizing a Trainium2 kernel written in Bass

```python
import numpy as np
import jax
import jax.numpy as jnp

def _softmax(x, axis=-1):
    return jax.nn.softmax(x, axis=axis)

def _gelu(x):
    return jax.nn.gelu(x, approximate=True)

def _silu(x):
    return jax.nn.silu(x)

def _sigmoid(x):
    return jax.nn.sigmoid(x)

def _layernorm(x, axis=-1, eps=1e-05):
    m = jnp.mean(x, axis=axis, keepdims=True)
    v = jnp.var(x, axis=axis, keepdims=True)
    return (x - m) / jnp.sqrt(v + eps)

def _scatter_add(tgt, idx, src, axis=0):
    return tgt.at[idx].add(src)

def _segment_sum(src, seg, n):
    return jax.ops.segment_sum(src, seg, n)
kernel_name = 'mk_adj_ffn_d1_adj_r2_8495fe'

def setup_inputs(seed: int=0):
    np.random.seed(seed)
    _w = jnp.asarray

    def _rec_inputs():
        import jax
        import jax.numpy as jnp
        _gk = jax.random.key(seed)
        x = -0.000929 + 1 * jax.random.normal(jax.random.fold_in(_gk, 1), (128, 128, 128), jnp.float32)
        _w = (1.0 + jnp.arange(128, dtype=jnp.float32)) ** (-0.5)
        _w = _w / _w.mean()
        _pij = jnp.clip(0.0625 * _w[:, None] * _w[None, :], 0.0, 1.0)
        _a = jax.random.uniform(jax.random.fold_in(_gk, 2), (128, 128, 128)) < _pij
        _a = jnp.logical_or(_a, jnp.eye(128, dtype=bool))
        _af = _a.astype(jnp.float32)
        adj = _af
        return (x, adj)
    x, adj = _rec_inputs()

    def _L0_gnn_setup():
        import jax, jax.numpy as jnp
        import numpy as np
        B, N = (1, 2048)
        D_IN, D_OUT, H = (128, 128, 8)
        HD = D_OUT // H
        NEG = -9000000000000000.0

        def _xavier(key, shape):
            lim = np.sqrt(6.0 / (shape[0] + shape[1])).astype(np.float32)
            return jax.random.uniform(key, shape, jnp.float32, -lim, lim)
        key = jax.random.key(seed)
        ks = jax.random.split(key, 8)
        x = jax.random.normal(ks[0], (B, N, D_IN), jnp.float32)
        adj = (jax.random.uniform(ks[1], (B, N, N)) < 0.05).astype(jnp.float32)
        idx = jnp.arange(N)
        adj = adj.at[:, idx, idx].set(1.0)
        Wq = _xavier(ks[2], (D_IN, D_OUT))
        bq = jnp.zeros((D_OUT,), jnp.float32)
        Wk = _xavier(ks[3], (D_IN, D_OUT))
        bk = jnp.zeros((D_OUT,), jnp.float32)
        Wv = _xavier(ks[4], (D_IN, D_OUT))
        bv = jnp.zeros((D_OUT,), jnp.float32)
        Wo = _xavier(ks[5], (D_OUT, D_OUT))
        bo = jnp.zeros((D_OUT,), jnp.float32)
        return dict(x=x, adj=adj, Wq=Wq, bq=bq, Wk=Wk, bk=bk, Wv=Wv, bv=bv, Wo=Wo, bo=bo)
    _L0_gnn_all = _L0_gnn_setup()
    _L0_gnn_in = {k: v for k, v in _L0_gnn_all.items() if k in ('Wq', 'bq', 'Wk', 'bk', 'Wv', 'bv', 'Wo', 'bo')}
    del _L0_gnn_all

    def _L0_ffn_setup():
        import jax, jax.numpy as jnp
        import numpy as np
        B, S, D, F, E, K = (8, 1024, 128, 512, 8, 2)
        key = jax.random.key(seed)
        ks = jax.random.split(key, 10)
        s = 0.02
        return {'x': jax.random.normal(ks[0], (B, S, D), dtype=jnp.float32), 'Wr': jax.random.normal(ks[1], (D, E), dtype=jnp.float32) * s, 'W1s': jax.random.normal(ks[2], (D, F), dtype=jnp.float32) * s, 'b1s': jnp.zeros((F,), dtype=jnp.float32), 'W2s': jax.random.normal(ks[3], (F, D), dtype=jnp.float32) * s, 'b2s': jnp.zeros((D,), dtype=jnp.float32), 'W1p': jax.random.normal(ks[4], (E, D, F), dtype=jnp.float32) * s, 'b1p': jnp.zeros((E, F), dtype=jnp.float32), 'W2p': jax.random.normal(ks[5], (E, F, D), dtype=jnp.float32) * s, 'b2p': jnp.zeros((E, D), dtype=jnp.float32)}
    _L0_ffn_all = _L0_ffn_setup()
    _L0_ffn_in = {k: v for k, v in _L0_ffn_all.items() if k in ('Wr', 'W1s', 'b1s', 'W2s', 'b2s', 'W1p', 'b1p', 'W2p', 'b2p')}
    del _L0_ffn_all
    return {'x': x, 'adj': adj, 'L0_gnn_Wq': _L0_gnn_in['Wq'], 'L0_gnn_bq': _L0_gnn_in['bq'], 'L0_gnn_Wk': _L0_gnn_in['Wk'], 'L0_gnn_bk': _L0_gnn_in['bk'], 'L0_gnn_Wv': _L0_gnn_in['Wv'], 'L0_gnn_bv': _L0_gnn_in['bv'], 'L0_gnn_Wo': _L0_gnn_in['Wo'], 'L0_gnn_bo': _L0_gnn_in['bo'], 'L0_ffn_Wr': _L0_ffn_in['Wr'], 'L0_ffn_W1s': _L0_ffn_in['W1s'], 'L0_ffn_b1s': _L0_ffn_in['b1s'], 'L0_ffn_W2s': _L0_ffn_in['W2s'], 'L0_ffn_b2s': _L0_ffn_in['b2s'], 'L0_ffn_W1p': _L0_ffn_in['W1p'], 'L0_ffn_b1p': _L0_ffn_in['b1p'], 'L0_ffn_W2p': _L0_ffn_in['W2p'], 'L0_ffn_b2p': _L0_ffn_in['b2p']}

def reference(x, adj, L0_gnn_Wq, L0_gnn_bq, L0_gnn_Wk, L0_gnn_bk, L0_gnn_Wv, L0_gnn_bv, L0_gnn_Wo, L0_gnn_bo, L0_ffn_Wr, L0_ffn_W1s, L0_ffn_b1s, L0_ffn_W2s, L0_ffn_b2s, L0_ffn_W1p, L0_ffn_b1p, L0_ffn_W2p, L0_ffn_b2p):
    import jax
    import jax.numpy as jnp

    def _L0_gnn_ref(x, adj, Wq, bq, Wk, bk, Wv, bv, Wo, bo):
        import jax, jax.numpy as jnp
        import numpy as np
        B, N = (1, 2048)
        D_IN, D_OUT, H = (128, 128, 8)
        HD = D_OUT // H
        NEG = -9000000000000000.0

        def _xavier(key, shape):
            lim = np.sqrt(6.0 / (shape[0] + shape[1])).astype(np.float32)
            return jax.random.uniform(key, shape, jnp.float32, -lim, lim)
        b, n, _ = x.shape

        def split_heads(t):
            return t.reshape(b, n, H, HD).transpose(0, 2, 1, 3)
        q = split_heads(x @ Wq + bq)
        k = split_heads(x @ Wk + bk)
        v = split_heads(x @ Wv + bv)
        scores = jnp.einsum('bhqd,bhkd->bhqk', q, k) / np.float32(np.sqrt(HD))
        scores = jnp.where(adj[:, None, :, :] > 0, scores, jnp.float32(NEG))
        attn = jax.nn.softmax(scores, axis=-1)
        out = jnp.einsum('bhqk,bhkd->bhqd', attn, v)
        out = out.transpose(0, 2, 1, 3).reshape(b, n, D_OUT)
        return out @ Wo + bo

    def _L0_ffn_ref(x, Wr, W1s, b1s, W2s, b2s, W1p, b1p, W2p, b2p):
        import jax, jax.numpy as jnp
        import numpy as np
        B, S, D, F, E, K = (8, 1024, 128, 512, 8, 2)
        gelu = lambda t: jax.nn.gelu(t, approximate=False)
        shared = gelu(x @ W1s + b1s) @ W2s + b2s
        rw = jax.nn.softmax(x @ Wr, axis=-1)
        topw, topi = jax.lax.top_k(rw, K)
        topw = topw / jnp.sum(topw, axis=-1, keepdims=True)
        mask = jnp.sum(jax.nn.one_hot(topi, E, dtype=topw.dtype) * topw[..., None], axis=-2)
        h = gelu(jnp.einsum('bsd,edf->bsef', x, W1p) + b1p)
        priv = jnp.einsum('bsef,efd->bsed', h, W2p) + b2p
        routed = jnp.einsum('bsed,bse->bsd', priv, mask)
        return shared + routed
    x = x + _L0_gnn_ref(_layernorm(x, axis=-1), adj, L0_gnn_Wq, L0_gnn_bq, L0_gnn_Wk, L0_gnn_bk, L0_gnn_Wv, L0_gnn_bv, L0_gnn_Wo, L0_gnn_bo)
    x = x + _L0_ffn_ref(_layernorm(x, axis=-1), L0_ffn_Wr, L0_ffn_W1s, L0_ffn_b1s, L0_ffn_W2s, L0_ffn_b2s, L0_ffn_W1p, L0_ffn_b1p, L0_ffn_W2p, L0_ffn_b2p)
    return x

_drawn_inputs = setup_inputs


def setup_inputs(seed=0):
    import zlib

    import numpy as np

    out = dict(_drawn_inputs(seed))
    spreads = {'L0_gnn_bq': (0.0, 0.1),
     'L0_gnn_bk': (0.0, 0.8),
     'L0_gnn_bv': (0.0, 0.1),
     'L0_gnn_bo': (0.0, 0.1),
     'L0_ffn_b1s': (0.0, 0.386),
     'L0_ffn_b2s': (0.0, 0.1),
     'L0_ffn_b1p': (0.0, 0.521),
     'L0_ffn_b2p': (0.0, 0.1)}
    factors = {}
    for name, (base, spread) in spreads.items():
        noise = np.random.default_rng([zlib.crc32(name.encode()), seed]).standard_normal(out[name].shape)
        drawn = base * np.exp(spread * noise) if base else spread * noise
        out[name] = jnp.asarray(drawn.astype(out[name].dtype))
    for name, factor in factors.items():
        out[name] = (out[name] * factor).astype(out[name].dtype)
    return out
```

```python
from contextlib import ExitStack

import concourse.bass as bass
from concourse import mybir

ALU = mybir.AluOpType
ACT = mybir.ActivationFunctionType
AX_X = mybir.AxisListType.X
F32 = mybir.dt.float32
F16 = mybir.dt.float16
BF16 = mybir.dt.bfloat16

P = 128
NT = 128
GT = 4
NG = NT // GT
H = 8
HD = 16
VW = HD + 1
NEG = -9000000000000000.0
EPS = 1e-5
E = 8
EA = E + 1
FC = 4
F = FC * P

XS = 64.0
WS = 64.0
HS = 16.0


def attention_phase(nc, ctx, d, x_res, xT_res, logits):
    def sb(name, shape, dt=F32):
        return ctx.enter_context(nc.sbuf_tensor(name, shape, dt))

    def ps(name, shape, dt=F32):
        return ctx.enter_context(nc.psum_tensor(name, shape, dt))

    def sem(name):
        return ctx.enter_context(nc.semaphore(name))

    ident = sb("ident", [P, P])
    ident16 = sb("ident16", [P, P], F16)
    identb = sb("identb", [P, P], BF16)
    ones = sb("ones", [P, P])
    wq, wk, wv, wo = (sb(n, [P, P]) for n in ("wq", "wk", "wv", "wo"))
    wr = sb("wr", [P, E])
    wr64 = sb("wr64", [P, E])
    wr16 = sb("wr16", [P, 2, E], F16)
    cols = sb("cols", [P, 3])
    parity = sb("parity", [P, 2])
    qb = sb("qb", [P, 1])
    kb = sb("kb", [P, 2])
    bv_mat = sb("bv_mat", [P, P])
    bo_rows = sb("bo_rows", [P, P])
    out_bias = sb("out_bias", [P, P])
    adj = sb("adj", [P, 2, GT, P])
    negmask = sb("negmask", [P, 2, GT, P], BF16)
    xn = sb("xn", [P, GT, P])
    xnT = sb("xnT", [P, GT * P])
    QT = sb("QT", [P, 2, GT * P])
    KT = sb("KT", [P, 2, 2, GT * P])
    V = sb("V", [P, 2, GT, H, VW])
    probs = sb("probs", [P, 2, H, P])
    probsT = sb("probsT", [P, H, P])
    attn = sb("attn", [P, GT, H, HD])
    attnT = sb("attnT", [P, GT * P])
    xc = sb("xc", [P, GT, P])
    xc2 = sb("xc2", [P, GT, P])
    xs2 = sb("xs2", [P, GT, P])
    x16 = sb("x16", [P, 2, GT, P], F16)
    bn1 = sb("bn1", [P, GT, 6])
    mv1 = sb("mv1", [P, 2, GT, 2])
    rs1 = sb("rs1", [P, 2, GT])
    bn2 = sb("bn2", [P, GT, 6])
    mv2 = sb("mv2", [P, GT, 2])
    ve1 = sb("ve1", [P, 2, GT])
    ve2 = sb("ve2", [P, GT])
    half = sb("half", [P, GT])
    rs2s = sb("rs2s", [P, GT])
    smax = sb("smax", [P, H])
    turn = sb("turn_dve", [P, 1])
    rden = sb("rden", [P, H])

    S = ps("S", [P, 4, 512])
    PT = ps("PT", [P, H, P])
    PV = ps("PV", [P, 512])
    M0 = ps("M0", [P, 512])
    M16 = M0[:, :].bitcast(F16).rearrange("p (a t) -> p a t", a=2)
    S_heads = S[:, :, 0:2 * P].rearrange("p r (e k) -> p r e k", e=2)
    PVh = PV[:, 0:H * VW].rearrange("p (h c) -> p h c", h=H)

    consts = sem("consts")
    prep = sem("prep")
    bias_ps = sem("bias_ps")
    loaded = [sem("loaded0"), sem("loaded1")]
    names = ["bn1_done", "aggr1", "ln1_stats", "xn_ready", "mask_ready", "bias_added", "xT_ps", "xT_sb", "q_ps", "q_sb",
             "k_ps", "k_sb", "v_ps", "v_sb", "aT_ps", "aT_sb", "out_ps", "x2_done", "bn2_done", "aggr2", "rs1_done", "rs2_done", "xc1_done", "xc2_done",
             "ln2_stats", "xs2_done", "hi_done", "split_done", "x2T_ps", "x2T_sb", "lg_ps", "lg_sb",
             "s_ps", "max_done", "sub_done", "exp_done", "pt_ps", "pt_sb", "pv_ps", "rec_done", "norm_done"]
    s = {n: sem(n) for n in names}

    def wait(eng, name, count):
        if not (isinstance(count, int) and count <= 0):
            eng.wait_ge(s[name], count)

    def set_up(eng, g):
        if not isinstance(g, int):
            eng.wait_ge(prep, 4)

    def has(g, off=0, n=NG):
        return not isinstance(g, int) or 0 <= g - off < n

    M0_ORDER = [("xT", -1, "xT_sb"), ("Q", -1, "q_sb"), ("K", -1, "k_sb"), ("V", -1, "v_sb"),
                ("x2T", 2, "x2T_sb"), ("aT", 1, "aT_sb"), ("lg", 2, "lg_sb"), ("out", 1, "x2_done")]

    def m0_free(pe, task, g):
        at = [t[0] for t in M0_ORDER].index(task)
        while True:
            at -= 1
            if at < 0:
                at, g = len(M0_ORDER) - 1, g - 1
                if isinstance(g, int) and g < -1:
                    return
            _, off, emptied = M0_ORDER[at]
            if has(g, off):
                wait(pe, emptied, g - off + 1)
                return

    NCONST = 11
    nc_block = ctx.enter_context(nc.Block())

    @nc_block.sync
    def _(sp):
        for dst, src in ((ident[:], d["ident"]), (parity[:], d["parity"]), (wq[:], d["Wq"]), (wk[:], d["Wk"]),
                         (wv[:], d["Wv"]), (wo[:], d["Wo"]), (wr[:], d["Wr"]),
                         (cols[:, 0:1], d["bq"].unsqueeze(1)), (cols[:, 1:2], d["bk"].unsqueeze(1)),
                         (cols[:, 2:3], d["bv"].unsqueeze(1)),
                         (bo_rows[:], d["bo"].unsqueeze(0).to_broadcast([P, P]))):
            sp.dma_start(dst, src).then_inc(consts, 16)

        def load(g, q):
            wait(sp, "mask_ready", g - 1)
            sp.dma_start(x_res[:, bass.ds(g * GT, GT), :],
                         d["x"][bass.ds(g * GT, GT)].rearrange("b t c -> t b c")).then_inc(loaded[q], 16)
            sp.dma_start(adj[:, q], d["adj"][bass.ds(g * GT, GT)].rearrange("b t c -> t b c")).then_inc(loaded[q], 16)

        load(0, 0)
        load(1, 1)
        with sp.Fori(1, NG // 2) as r:
            load(2 * r, 0)
            load(2 * r + 1, 1)

    def pair_blocks(eng, step):
        step(-1, 1)
        step(0, 0)
        step(1, 1)
        with eng.Fori(1, NG // 2 - 1) as r:
            step(2 * r, 0)
            step(2 * r + 1, 1)
        step(NG - 2, 0)
        step(NG - 1, 1)
        step(NG, 0)
        step(NG + 1, 1)

    @nc_block.gpsimd
    def _(pool):
        pool.wait_ge(consts, 16 * NCONST)
        pool.memset(ones[:], 1.0).then_inc(prep, 1)
        pool.memset(V[:, :, :, :, HD:VW], 1.0).then_inc(prep, 1)
        pool.memset(half[:], -0.5)
        pool.tensor_copy(ident16[:], ident[:]).then_inc(prep, 1)
        pool.tensor_copy(identb[:], ident[:]).then_inc(prep, 1)

        def norm1(g, q):
            wait(pool, "ln1_stats", g + 1)
            wait(pool, "xT_ps", g)
            pool.tensor_tensor(rs1[:, q], ve1[:, q], half[:], ALU.pow).then_inc(s["rs1_done"], 1)
            xg = x_res[:, bass.ds(g * GT, GT), :]
            pool.wait_ge(s["rs1_done"], 1)
            pool.tensor_tensor(xc[:], xg, mv1[:, q, :, 0:1].to_broadcast([P, GT, P]),
                               ALU.subtract).then_inc(s["xc1_done"], 1)
            wait(pool, "rs1_done", g + 1)
            wait(pool, "xc1_done", g + 1)
            pool.tensor_tensor(xn[:], xc[:], rs1[:, q].unsqueeze(2).to_broadcast([P, GT, P]),
                               ALU.mult).then_inc(s["xn_ready"], 1)
            set_up(pool, g)
            wait(pool, "xn_ready", g + 1)
            if isinstance(g, int) and g == 0:
                pool.wait_ge(prep, 11)
            pool.tensor_tensor(xg, xg, out_bias[:].unsqueeze(1).to_broadcast([P, GT, P]),
                               ALU.add).then_inc(s["bias_added"], 1)

        def split(g):
            wait(pool, "ln2_stats", g + 1)
            wait(pool, "split_done", g)
            pool.tensor_tensor(rs2s[:], ve2[:], half[:], ALU.pow).then_inc(s["rs2_done"], 1)
            pool.tensor_tensor(xc2[:], x_res[:, bass.ds(g * GT, GT), :], mv2[:, :, 0:1].to_broadcast([P, GT, P]),
                               ALU.subtract).then_inc(s["xc2_done"], 1)
            wait(pool, "rs2_done", g + 1)
            wait(pool, "xc2_done", g + 1)
            pool.tensor_tensor(xs2[:], xc2[:], rs2s[:].unsqueeze(2).to_broadcast([P, GT, P]),
                               ALU.mult).then_inc(s["xs2_done"], 1)
            set_up(pool, g)
            wait(pool, "x2T_ps", g)
            wait(pool, "xs2_done", g + 1)
            pool.tensor_copy(x16[:, 0], xs2[:]).then_inc(s["hi_done"], 1)
            wait(pool, "hi_done", g + 1)
            pool.tensor_tensor(x16[:, 1], xs2[:], x16[:, 0], ALU.subtract).then_inc(s["split_done"], 1)

        def step(g, q):
            if isinstance(g, int) and g == -1:
                norm1(0, 0)
            if has(g, -2):
                norm1(g + 2, q)
            if has(g, 2):
                split(g - 2)

        pair_blocks(pool, step)

    @nc_block.vector
    def _(dve):
        dve.wait_ge(consts, 16 * NCONST)
        dve.wait_ge(prep, 4)
        dve.tensor_scalar(wr64[:], wr[:], WS, None, ALU.mult).then_inc(prep, 1)
        dve.tensor_scalar(bv_mat[:], ones[:], cols[:, 2:3], None, ALU.mult).then_inc(prep, 1)
        dve.tensor_scalar(qb[:], cols[:, 0:1], 0.25, None, ALU.mult).then_inc(prep, 1)
        dve.tensor_scalar(kb[:], parity[:], cols[:, 1:2], None, ALU.mult).then_inc(prep, 1)
        dve.wait_ge(prep, 8)
        dve.tensor_copy(wr16[:, 0], wr64[:]).then_inc(prep, 1)
        dve.wait_ge(prep, 9)
        dve.tensor_tensor(wr16[:, 1], wr64[:], wr16[:, 0], ALU.subtract).then_inc(prep, 1)
        dve.wait_ge(bias_ps, 1)
        dve.tensor_tensor(out_bias[:], M0[:, 0:P], bo_rows[:], ALU.add).then_inc(prep, 1)

        def stats1(g, q):
            set_up(dve, g)
            dve.wait_ge(loaded[q], (g // 2 + 1) * 32 if isinstance(g, int) else (g - q) * 16 + 32)
            wait(dve, "xn_ready", g - 1)
            wait(dve, "aggr1", g)
            for j in range(GT):
                last = dve.bn_stats(bn1[:, j, :], x_res[:, g * GT + j, :])
            last.then_inc(s["bn1_done"], 1)
            wait(dve, "bn1_done", g + 1)
            if not isinstance(g, int):
                dve.memset(turn[:], 0.0)
            for j in range(GT):
                last = dve.bn_aggr(mv1[:, q, j, :], bn1[:, j, :])
            last.then_inc(s["aggr1"], 1)
            wait(dve, "aggr1", g + 1)
            dve.tensor_scalar(ve1[:, q], mv1[:, q, :, 1], EPS, None, ALU.add).then_inc(s["ln1_stats"], 1)

        def mask(g, q):
            dve.wait_ge(loaded[q], (g // 2 + 1) * 32 if isinstance(g, int) else (g - q) * 16 + 32)
            wait(dve, "s_ps", (g - 1) * GT if isinstance(g, int) else g * GT - GT)
            dve.tensor_scalar(negmask[:, q], adj[:, q], 0.0, NEG, ALU.is_le, ALU.mult).then_inc(s["mask_ready"], 1)

        def residual_and_stats2(g):
            wait(dve, "out_ps", g + 1)
            wait(dve, "bias_added", g + 1)
            xg = x_res[:, bass.ds(g * GT, GT), :]
            dve.tensor_tensor(xg, M0[:, :].rearrange("p (j c) -> p j c", j=GT), xg, ALU.add).then_inc(s["x2_done"], 1)
            set_up(dve, g)
            wait(dve, "x2_done", g + 1)
            wait(dve, "aggr2", g)
            for j in range(GT):
                last = dve.bn_stats(bn2[:, j, :], x_res[:, g * GT + j, :])
            last.then_inc(s["bn2_done"], 1)
            set_up(dve, g)
            wait(dve, "bn2_done", g + 1)
            wait(dve, "xs2_done", g)
            for j in range(GT):
                last = dve.bn_aggr(mv2[:, j, :], bn2[:, j, :])
            last.then_inc(s["aggr2"], 1)
            wait(dve, "aggr2", g + 1)
            dve.tensor_scalar(ve2[:], mv2[:, :, 1], EPS, 1.0 / (XS * XS), ALU.add, ALU.mult).then_inc(s["ln2_stats"], 1)

        def normalise(t, j):
            wait(dve, "pv_ps", t + 1)
            wait(dve, "norm_done", t)
            dve.reciprocal(rden[:], PVh[:, :, HD]).then_inc(s["rec_done"], 1)
            wait(dve, "rec_done", t + 1)
            if j == 0:
                wait(dve, "aT_ps", t // GT if isinstance(t, int) else t * 0 + t_group(t))
            dve.tensor_tensor(attn[:, j], PVh[:, :, 0:HD], rden[:].unsqueeze(2).to_broadcast([P, H, HD]),
                              ALU.mult).then_inc(s["norm_done"], 1)

        group_now = [0]

        def t_group(t):
            return group_now[0]

        def softmax_shift(t, b):
            wait(dve, "s_ps", t + 1)
            wait(dve, "sub_done", t)
            dve.tensor_reduce(smax[:].rearrange("p (r e) -> p r e", e=2), S_heads, AX_X, ALU.max).then_inc(s["max_done"], 1)
            wait(dve, "max_done", t + 1)
            wait(dve, "pt_ps", t - 1)
            dve.tensor_tensor(probs[:, b].rearrange("p (r e) k -> p r e k", e=2), S_heads,
                              smax[:].rearrange("p (r e) -> p r e", e=2).unsqueeze(3).to_broadcast([P, 4, 2, P]),
                              ALU.subtract).then_inc(s["sub_done"], 1)

        def step(g, q):
            if isinstance(g, int) and g == -1:
                stats1(0, 0)
                mask(0, 0)
                stats1(1, 1)
                return
            for j in range(GT):
                t = g * GT + j
                if has(t, 3, NT):
                    group_now[0] = g if j == 3 else g - 1
                    normalise(t - 3, (j - 3) % GT)
                if j == 0 and has(g, 2):
                    residual_and_stats2(g - 2)
                if j == 1 and has(g, -2):
                    stats1(g + 2, q)
                if j == 2 and has(g, -1):
                    mask(g + 1, 1 - q)
                if has(t, 0, NT):
                    softmax_shift(t, j % 2)

        pair_blocks(dve, step)

    @nc_block.scalar
    def _(act):
        act.wait_ge(prep, 8)

        def evac(task, g, q):
            if task == "xT":
                wait(act, "xT_ps", g + 1)
                act.activation(xnT[:], M0[:, :], ACT.Copy).then_inc(s["xT_sb"], 1)
            elif task == "Q":
                wait(act, "q_ps", g + 1)
                act.activation(QT[:, q], M0[:, :], ACT.Identity, bias=qb[:], scale=0.25).then_inc(s["q_sb"], 1)
            elif task == "K":
                wait(act, "k_ps", g + 1)
                act.activation(KT[:, q, 0], M0[:, :], ACT.Identity, bias=kb[:, 0:1], scale=parity[:, 0:1])
                act.activation(KT[:, q, 1], M0[:, :], ACT.Identity, bias=kb[:, 1:2],
                               scale=parity[:, 1:2]).then_inc(s["k_sb"], 1)
            elif task == "V":
                wait(act, "v_ps", g + 1)
                act.activation(V[:, q, :, :, 0:HD].rearrange("p j h c -> p (j h) c"),
                               M0[:, :].rearrange("p (j c) -> p j c", c=HD), ACT.Copy).then_inc(s["v_sb"], 1)
            elif task == "aT":
                wait(act, "aT_ps", g + 1)
                act.activation(attnT[:], M0[:, :], ACT.Copy).then_inc(s["aT_sb"], 1)
            elif task == "x2T":
                set_up(act, g)
                wait(act, "x2T_ps", g + 1)
                act.activation(xT_res[:, :, bass.ds(g * GT * P, GT * P)], M16, ACT.Copy).then_inc(s["x2T_sb"], 1)
            elif task == "lg":
                set_up(act, g)
                wait(act, "lg_ps", g + 1)
                act.activation(logits[:, bass.ds(g * GT, GT), :], M0[:, 0:GT * E].rearrange("p (j e) -> p j e", e=E),
                               ACT.Copy, scale=1.0 / (XS * WS)).then_inc(s["lg_sb"], 1)

        def slot_tasks(g, q, j):
            a, b = {0: (("xT", g + 1, 1 - q), ("Q", g + 1, 1 - q)), 1: (("K", g + 1, 1 - q), ("V", g + 1, 1 - q)),
                    2: (("x2T", g - 2, q), ("aT", g - 1, 1 - q)), 3: (("lg", g - 2, q), None)}[j]
            return a, b

        def step(g, q):
            for j in range(GT):
                t = g * GT + j
                a, b = slot_tasks(g, q, j)
                if has(t, 1, NT):
                    wait(act, "sub_done", t)
                    pr = probs[:, (j - 1) % 2]
                    act.activation(pr, pr, ACT.Exp).then_inc(s["exp_done"], 1)
                if has(a[1]):
                    evac(*a)
                if has(t, 1, NT):
                    wait(act, "pt_ps", t)
                    wait(act, "pv_ps", t - 1)
                    act.activation(probsT[:], PT[:, :, :], ACT.Copy).then_inc(s["pt_sb"], 1)
                if b and has(b[1]):
                    evac(*b)

        pair_blocks(act, step)

    @nc_block.tensor
    def _(pe):
        pe.wait_ge(prep, 8)
        pe.matmul(M0[:, 0:P], bv_mat[:], wo[:], start=True, stop=True).then_inc(bias_ps, 1)
        pe.wait_ge(prep, 11)

        def m0_task(task, g, q, step_g):
            if task == "xT":
                wait(pe, "xn_ready", g + 1)
                m0_free(pe, task, step_g)
                for j in range(GT):
                    mm = pe.transpose(M0[:, j * P:(j + 1) * P], xn[:, j], ident[:])
                mm.then_inc(s["xT_ps"], 1)
            elif task in "QK":
                m0_free(pe, task, step_g)
                mm = pe.matmul(M0[:, :], (wq if task == "Q" else wk)[:], xnT[:], start=True, stop=True)
                mm.then_inc(s["q_ps" if task == "Q" else "k_ps"], 1)
            elif task == "V":
                m0_free(pe, task, step_g)
                for j in range(GT):
                    mm = pe.matmul(M0[:, j * P:(j + 1) * P], xnT[:, j * P:(j + 1) * P], wv[:], start=True, stop=True)
                mm.then_inc(s["v_ps"], 1)
            elif task == "aT":
                wait(pe, "norm_done", (g + 1) * GT)
                m0_free(pe, task, step_g)
                for j in range(GT):
                    mm = pe.transpose(M0[:, j * P:(j + 1) * P], attn[:, j].rearrange("p h c -> p (h c)"), ident[:])
                mm.then_inc(s["aT_ps"], 1)
            elif task == "out":
                wait(pe, "aT_sb", g + 1)
                m0_free(pe, task, step_g)
                for j in range(GT):
                    mm = pe.matmul(M0[:, j * P:(j + 1) * P], attnT[:, j * P:(j + 1) * P], wo[:], start=True, stop=True)
                mm.then_inc(s["out_ps"], 1)
            elif task == "x2T":
                wait(pe, "split_done", g + 1)
                m0_free(pe, task, step_g)
                for part in range(2):
                    for j in range(GT):
                        mm = pe.transpose(M16[:, part, j * P:(j + 1) * P], x16[:, part, j], ident16[:])
                mm.then_inc(s["x2T_ps"], 1)
            elif task == "lg":
                wait(pe, "x2T_sb", g + 1)
                m0_free(pe, task, step_g)
                for j in range(GT):
                    for n, (a, b) in enumerate(((0, 0), (0, 1), (1, 0))):
                        mm = pe.matmul(M0[:, j * E:(j + 1) * E], xT_res[:, a, bass.ds((g * GT + j) * P, P)],
                                       wr16[:, b], start=n == 0, stop=n == 2)
                mm.then_inc(s["lg_ps"], 1)

        def step(g, q):
            for j in range(GT):
                t = g * GT + j
                tasks = {0: (("xT", g + 1, 1 - q), ("Q", g + 1, 1 - q)), 1: (("K", g + 1, 1 - q), ("V", g + 1, 1 - q)),
                         2: (("x2T", g - 2, q), ("aT", g - 1, 1 - q)), 3: (("lg", g - 2, q), ("out", g - 1, 1 - q))}[j]
                if has(t, 0, NT):
                    if j == 0:
                        wait(pe, "k_sb", g + 1)
                        wait(pe, "mask_ready", g + 1)
                    wait(pe, "sub_done", t)
                    for r in range(4):
                        rows = slice(32 * r, 32 * r + 32)
                        pe.matmul(S_heads[:, r], QT[rows, q, j * P:(j + 1) * P], KT[rows, q, :, j * P:(j + 1) * P],
                                  start=True, stop=False)
                    for r in range(4):
                        mm = pe.matmul(S_heads[:, r], identb[:], negmask[:, q, j].unsqueeze(1).to_broadcast([P, 2, P]),
                                       start=False, stop=True)
                    mm.then_inc(s["s_ps"], 1)
                if has(t, 2, NT):
                    vq, vj = (q, j - 2) if j >= 2 else (1 - q, j + 2)
                    if vj == 0:
                        wait(pe, "v_sb", g + 1)
                    wait(pe, "pt_sb", t - 1)
                    wait(pe, "norm_done", t - 2)
                    for h in range(H):
                        mm = pe.matmul(PVh[:, h], probsT[:, h], V[:, vq, vj, h], start=True, stop=True)
                    mm.then_inc(s["pv_ps"], 1)
                if has(tasks[0][1]):
                    m0_task(*tasks[0], g)
                if has(t, 1, NT):
                    wait(pe, "exp_done", t)
                    wait(pe, "pt_sb", t - 1)
                    for h in range(H):
                        mm = pe.transpose(PT[:, h], probs[:, (j - 1) % 2, h], ident[:])
                    mm.then_inc(s["pt_ps"], 1)
                if has(tasks[1][1]):
                    m0_task(*tasks[1], g)

        pair_blocks(pe, step)


def router_phase(nc, ctx, d, logits, mask, mask_y):
    def sb(name, shape, dt=F32):
        return ctx.enter_context(nc.sbuf_tensor(name, shape, dt))

    rank_key = sb("rank_key", [P, E])
    eq = sb("eq", [P, NT, E])
    pick1 = sb("pick1", [P, NT, E])
    pick2 = sb("pick2", [P, NT, E])
    rest = sb("rest", [P, NT, E])
    m1, m2, key, diff, e2, den, w1, w2 = (sb(f"rt_{n}", [P, NT]) for n in "abcdefgh")
    key_loaded = ctx.enter_context(nc.semaphore("key_loaded"))
    routed = ctx.enter_context(nc.semaphore("routed"))
    diff_ready = ctx.enter_context(nc.semaphore("diff_ready"))
    exp2_ready = ctx.enter_context(nc.semaphore("exp2_ready"))
    block = ctx.enter_context(nc.Block())

    def wide(v):
        return v[:].unsqueeze(2).to_broadcast([P, NT, E])

    @block.sync
    def _(sp):
        sp.dma_start(rank_key[:], d["rank_key"].unsqueeze(0).to_broadcast([P, E])).then_inc(key_loaded, 16)

    @block.scalar
    def _(act):
        act.wait_ge(diff_ready, 1)
        act.activation(e2[:], diff[:], ACT.Exp).then_inc(exp2_ready, 1)

    @block.vector
    def _(dve):
        steps = [0]

        def then(ins):
            steps[0] += 1
            ins.then_inc(routed, 1)
            dve.wait_ge(routed, steps[0])

        keys = rank_key[:].unsqueeze(1).to_broadcast([P, NT, E])
        dve.wait_ge(key_loaded, 16)
        for src, top, pick in ((logits, m1, pick1), (rest, m2, pick2)):
            then(dve.tensor_reduce(top[:], src[:], AX_X, ALU.max))
            then(dve.tensor_tensor(eq[:], src[:], wide(top), ALU.is_equal))
            then(dve.tensor_tensor(eq[:], eq[:], keys, ALU.mult))
            then(dve.tensor_reduce(key[:], eq[:], AX_X, ALU.max))
            then(dve.tensor_tensor(pick[:], wide(key), keys, ALU.is_equal))
            if pick is pick1:
                then(dve.scalar_tensor_tensor(out=rest[:], in0=pick1[:], scalar=-3.0e38, in1=logits[:],
                                              op0=ALU.mult, op1=ALU.add))
        dve.tensor_tensor(diff[:], m2[:], m1[:], ALU.subtract).then_inc(diff_ready, 1)
        dve.wait_ge(exp2_ready, 1)
        then(dve.tensor_scalar(den[:], e2[:], 1.0, None, ALU.add))
        then(dve.reciprocal(w1[:], den[:]))
        then(dve.tensor_tensor(w2[:], e2[:], w1[:], ALU.mult))
        then(dve.tensor_tensor(pick1[:], pick1[:], wide(w1), ALU.mult))
        then(dve.tensor_tensor(pick2[:], pick2[:], wide(w2), ALU.mult))
        then(dve.tensor_tensor(mask[:, :, 0:E], pick1[:], pick2[:], ALU.add))
        then(dve.memset(mask[:, :, E:EA], 1.0))
        then(dve.tensor_scalar(mask_y[:], mask[:], 1.0 / (HS * WS), None, ALU.mult))


def ffn_phase(nc, ctx, d, x_res, xT_res, mask, mask_y, out):
    def sb(name, shape, dt=F32):
        return ctx.enter_context(nc.sbuf_tensor(name, shape, dt))

    def ps(name, shape, dt=F32):
        return ctx.enter_context(nc.psum_tensor(name, shape, dt))

    def sem(name):
        return ctx.enter_context(nc.semaphore(name))

    w1 = sb("w1", [P, 2, EA, F], F16)
    w2 = sb("w2", [P, 2, EA, FC, P], F16)
    stage = sb("stage", [P, 2, F])
    b1 = sb("b1", [P, EA, FC])
    b1_rows = sb("b1_rows", [EA * FC, P])
    b2 = sb("b2", [EA, P])
    hid = sb("hid", [P, FC, F])
    h16 = sb("h16", [P, 2, 2, FC, F], F16)
    identc = sb("identc", [P, P])
    turn = sb("turn", [P, 1])
    maskT = hid[0:EA, 0, :]
    Z = ps("Z", [P, FC, F])
    Y = ps("Y", [P, 2, GT, P])
    MT_all = ps("MT", [P, GT * P])
    MT = MT_all[0:EA, :]
    BI = ps("BI", [P, GT, P])

    w_loaded = [sem("w_loaded0"), sem("w_loaded1")]
    b_loaded = sem("b_loaded")
    w_scaled, w_hi, w_split = sem("w_scaled"), sem("w_hi"), sem("w_split")
    mt_ps, mt_sb, bias_ps, bias_done = sem("mt_ps"), sem("mt_sb"), sem("bias2_ps"), sem("bias2_done")
    z_ps, gelu_done, hi_done, lo_done = sem("z_ps"), sem("gelu_done"), sem("hhi_done"), sem("hlo_done")
    b1_ps, b1_sb = sem("b1_ps"), sem("b1_sb")
    y_ps, y_added, stored = sem("y_ps"), sem("y_added"), sem("stored")
    block = ctx.enter_context(nc.Block())
    U = EA * NG

    w_src = [d["W1p"][e] for e in range(E)] + [d["W1s"]] + \
            [d["W2p"][e].rearrange("(c p) d -> p c d", p=P) for e in range(E)] + \
            [d["W2s"].rearrange("(c p) d -> p c d", p=P)]

    @block.sync
    def _(sp):
        sp.dma_start(identc[:], d["ident"]).then_inc(b_loaded, 16)
        sp.dma_start(b1_rows[0:E * FC], d["b1p"].rearrange("e (c p) -> (e c) p", p=P)).then_inc(b_loaded, 16)
        sp.dma_start(b1_rows[E * FC:EA * FC], d["b1s"].rearrange("(c p) -> c p", p=P)).then_inc(b_loaded, 16)
        sp.dma_start(b2[0:E], d["b2p"]).then_inc(b_loaded, 16)
        sp.dma_start(b2[E:EA], d["b2s"].unsqueeze(0)).then_inc(b_loaded, 16)
        for n, src in enumerate(w_src):
            if n >= 2:
                sp.wait_ge(w_split, n - 1)
            dst = stage[:, n % 2] if n < EA else stage[:, n % 2].rearrange("p (c d) -> p c d", c=FC)
            sp.dma_start(dst, src).then_inc(w_loaded[n % 2], 16)
        with sp.Fori(0, NG) as g:
            sp.wait_ge(y_added, g + (U - NG + 1))
            sp.dma_start(out[bass.ds(g * GT, GT)].rearrange("b t c -> t b c"),
                         x_res[:, bass.ds(g * GT, GT), :]).then_inc(stored, 16)
        sp.wait_ge(stored, 16 * NG)

    @block.gpsimd
    def _(pool):
        for n in range(len(w_src)):
            st = stage[:, n % 2]
            pool.wait_ge(w_loaded[n % 2], 16 * (n // 2 + 1))
            pool.tensor_scalar(st, st, WS, None, ALU.mult).then_inc(w_scaled, 1)
            hi, lo = (w1[:, k, n] if n < EA else w2[:, k, n - EA].rearrange("p c d -> p (c d)") for k in range(2))
            pool.wait_ge(w_scaled, n + 1)
            pool.tensor_copy(hi, st).then_inc(w_hi, 1)
            pool.wait_ge(w_hi, n + 1)
            pool.tensor_tensor(lo, st, hi, ALU.subtract).then_inc(w_split, 1)

    @block.tensor
    def _(pe):
        pe.wait_ge(b_loaded, 16 * 5)
        pe.transpose(MT_all[:, 0:EA * FC], b1_rows[:], identc[0:EA * FC, 0:EA * FC]).then_inc(b1_ps, 1)
        pe.wait_ge(b1_sb, 1)

        for g in range(NG):
            if g:
                pe.wait_ge(mt_sb, g)
            for j in range(GT):
                mm = pe.transpose(MT[:, j * P:(j + 1) * P], mask[:, g * GT + j], identc[:])
            mm.then_inc(mt_ps, 1)
            pe.wait_ge(mt_sb, g + 1)
            if g:
                pe.wait_ge(bias_done, g)
            for j in range(GT):
                mm = pe.matmul(BI[:, j], maskT[:, j * P:(j + 1) * P], b2[:], start=True, stop=True)
            mm.then_inc(bias_ps, 1)
        pe.wait_ge(w_split, len(w_src))

        def hidden(u, g, e):
            for c in range(FC):
                if not (isinstance(u, int) and u == 0):
                    pe.wait_ge(gelu_done, u * FC + (c + 1 - FC))
                for n, (a, b) in enumerate(((0, 0), (0, 1), (1, 0))):
                    mm = pe.matmul(Z[:, c], w1[:, a, :, c * P:(c + 1) * P][:, e, :],
                                   xT_res[:, b, bass.ds(g * GT * P, GT * P)], start=n == 0, stop=n == 2)
                mm.then_inc(z_ps, 1)

        def output(u, e, b):
            pe.wait_ge(lo_done, u * FC + FC)
            if not (isinstance(u, int) and u < 2):
                pe.wait_ge(y_added, u - 1)
            for j in range(GT):
                for c in range(FC):
                    for n, (k, m) in enumerate(((0, 0), (0, 1), (1, 0))):
                        mm = pe.matmul(Y[:, b, j], h16[:, b, k, c, j * P:(j + 1) * P], w2[:, m, e, c],
                                       start=c == 0 and n == 0, stop=c == FC - 1 and n == 2)
            mm.then_inc(y_ps, 1)

        hidden(0, 0, 0)
        hidden(1, 1, 0)
        output(0, 0, 0)
        hidden(2, 2, 0)
        output(1, 0, 1)
        with pe.Fori(1, U // 2 - 1) as r:
            u1 = 2 * r + 1
            hidden(u1, u1 % NG, u1 // NG)
            output(2 * r, (2 * r) // NG, 0)
            hidden(2 * r + 2, (2 * r + 2) % NG, (2 * r + 2) // NG)
            output(u1, u1 // NG, 1)
        hidden(U - 1, NG - 1, EA - 1)
        output(U - 2, EA - 1, 0)
        output(U - 1, EA - 1, 1)

    @block.scalar
    def _(act):
        act.wait_ge(b1_ps, 1)
        act.activation(b1[:].rearrange("p e c -> p (e c)"), MT_all[:, 0:EA * FC], ACT.Copy).then_inc(b1_sb, 1)
        for g in range(NG):
            act.wait_ge(mt_ps, g + 1)
            if g:
                act.wait_ge(bias_ps, g)
            act.activation(maskT, MT, ACT.Copy).then_inc(mt_sb, 1)

        def unit(u, e, b):
            first = isinstance(u, int) and u == 0

            def hi(c):
                act.wait_ge(gelu_done, u * FC + c + 1)
                if c == 0 and not (isinstance(u, int) and u < 2):
                    act.wait_ge(y_ps, u - 1)
                act.activation(h16[:, b, 0, c], hid[:, c], ACT.Copy, scale=HS).then_inc(hi_done, 1)

            for c in range(FC):
                act.wait_ge(z_ps, u * FC + c + 1)
                if not first:
                    act.wait_ge(lo_done, u * FC + (c + 1 - FC))
                if c:
                    hi(c - 1)
                else:
                    act.activation(turn[:], b1[:, 0, 0:1], ACT.Copy)
                act.activation(hid[:, c], Z[:, c], ACT.Gelu, bias=b1[:, e, c:c + 1],
                               scale=1.0 / (XS * WS)).then_inc(gelu_done, 1)
            hi(FC - 1)

        unit(0, 0, 0)
        unit(1, 0, 1)
        with act.Fori(1, U // 2) as r:
            unit(2 * r, (2 * r) // NG, 0)
            unit(2 * r + 1, (2 * r) // NG, 1)

    @block.vector
    def _(dve):
        for g in range(NG):
            dve.wait_ge(bias_ps, g + 1)
            xg = x_res[:, g * GT:(g + 1) * GT, :]
            dve.tensor_tensor(xg, BI[:], xg, ALU.add).then_inc(bias_done, 1)
        dve.wait_ge(bias_done, NG)

        def lows(u, b):
            for c in range(FC):
                dve.wait_ge(hi_done, u * FC + c + 1)
                dve.scalar_tensor_tensor(out=h16[:, b, 1, c], in0=hid[:, c], scalar=HS, in1=h16[:, b, 0, c],
                                         op0=ALU.mult, op1=ALU.subtract).then_inc(lo_done, 1)

        def add(u, g, e, b):
            dve.wait_ge(y_ps, u + 1)
            for j in range(GT):
                xt = x_res[:, g * GT + j, :]
                ins = dve.scalar_tensor_tensor(out=xt, in0=Y[:, b, j], scalar=mask_y[:, g * GT + j, :][:, bass.ds(e, 1)],
                                               in1=xt, op0=ALU.mult, op1=ALU.add)
            ins.then_inc(y_added, 1)

        lows(0, 0)
        lows(1, 1)
        add(0, 0, 0, 0)
        with dve.Fori(1, U // 2) as r:
            lows(2 * r, 0)
            pu = 2 * r - 1
            add(pu, pu % NG, pu // NG, 1)
            lows(2 * r + 1, 1)
            add(2 * r, (2 * r) % NG, (2 * r) // NG, 0)
        add(U - 1, NG - 1, EA - 1, 1)


def build(nc, d, out):
    with ExitStack() as whole:
        x_res = whole.enter_context(nc.sbuf_tensor("x_res", [P, NT, P], F32))
        xT_res = whole.enter_context(nc.sbuf_tensor("xT_res", [P, 2, NT * P], F16))
        logits = whole.enter_context(nc.sbuf_tensor("logits", [P, NT, E], F32))
        mask = whole.enter_context(nc.sbuf_tensor("mask", [P, NT, EA], F32))
        mask_y = whole.enter_context(nc.sbuf_tensor("mask_y", [P, NT, EA], F32))
        with ExitStack() as ctx:
            attention_phase(nc, ctx, d, x_res, xT_res, logits)
        with ExitStack() as ctx:
            router_phase(nc, ctx, d, logits, mask, mask_y)
        with ExitStack() as ctx:
            ffn_phase(nc, ctx, d, x_res, xT_res, mask, mask_y, out)


_INS = ["x", "adj"] + ["L0_gnn_" + n for n in ("Wq", "bq", "Wk", "bk", "Wv", "bv", "Wo", "bo")] + \
       ["L0_ffn_" + n for n in ("Wr", "W1s", "b1s", "W2s", "b2s", "W1p", "b1p", "W2p", "b2p")]


def kernel(**inputs):
    import numpy as _np
    import concourse.bacc as _bacc
    from concourse import mybir as _mybir
    from concourse.bass_utils import run_bass_kernel_spmd as _run

    nc = _bacc.Bacc("TRN2", target_bir_lowering=False, num_devices=1)
    arrays = {n: _np.ascontiguousarray(inputs[n]) for n in _INS}
    arrays["ident"] = _np.eye(P, dtype=_np.float32)
    even = (_np.arange(P) % 32 < HD).astype(_np.float32)
    arrays["parity"] = _np.stack([even, 1 - even], 1)
    arrays["rank_key"] = (E - _np.arange(E)).astype(_np.float32)
    fed, d = {}, {}
    for name, a in arrays.items():
        fed[f"in_{name}_dram"] = a
        d[name.split("_")[-1] if name != "rank_key" else name] = nc.dram_tensor(
            f"in_{name}_dram", a.shape, _mybir.dt.from_np(a.dtype), kind="ExternalInput").ap()
    out = nc.dram_tensor("out_0_dram", (NT, P, P), _mybir.dt.float32, kind="ExternalOutput").ap()
    build(nc, d, out)
    r = _run(nc, [fed], core_ids=[0])
    return r.results[0]["out_0_dram"]
```

```python
from contextlib import ExitStack

import concourse.bass as bass
from concourse import mybir

ALU = mybir.AluOpType
ACT = mybir.ActivationFunctionType
AX_X = mybir.AxisListType.X
F32 = mybir.dt.float32
U32 = mybir.dt.uint32
I32 = mybir.dt.int32
F16 = mybir.dt.float16
BF16 = mybir.dt.bfloat16

P = 128
NT = 128
GT = 4
NG = NT // GT
H = 8
HD = 16
VW = HD + 1
NEG = -9000000000000000.0
EPS = 1e-5
E = 8
EA = E + 1
FC = 4
F = FC * P

TOP = 2
SHARED = E
UT = GT * P
NU = TOP * NT * P // UT + E
ROW = P + 2

XS = 64.0
WS = 64.0
HS = 16.0
PS = 1024.0
VS = 16.0


def attention_phase(nc, ctx, d, x_res, x_rows, logits, xT_dram, slots_dram):
    def sb(name, shape, dt=F32):
        return ctx.enter_context(nc.sbuf_tensor(name, shape, dt))

    def ps(name, shape, dt=F32):
        return ctx.enter_context(nc.psum_tensor(name, shape, dt))

    def sem(name):
        return ctx.enter_context(nc.semaphore(name))

    ident = sb("ident", [P, P])
    ident16 = sb("ident16", [P, P], F16)
    identb = sb("identb", [P, P], BF16)
    ones = sb("ones", [P, P])
    wq, wk, wv, wo = (sb(n, [P, P]) for n in ("wq", "wk", "wv", "wo"))
    wr = sb("wr", [P, E])
    wr64 = sb("wr64", [P, E])
    wr16 = sb("wr16", [P, 2, E], F16)
    cols = sb("cols", [P, 3])
    parity = sb("parity", [P, 2])
    no_pair = sb("no_pair", [P, 1], U32)
    qb = sb("qb", [P, 1])
    kb = sb("kb", [P, 2])
    bv_mat = sb("bv_mat", [P, P])
    bo_rows = sb("bo_rows", [P, P])
    out_bias = sb("out_bias", [P, P])
    adj = sb("adj", [P, 2, GT, P])
    negmask = sb("negmask", [P, 2, GT, P], BF16)
    xn = sb("xn", [P, GT, P])
    xnT = sb("xnT", [P, GT * P])
    QT = sb("QT", [P, 2, GT * P])
    KT = sb("KT", [P, 2, 2, GT * P])
    V = sb("V", [P, 2, 2, GT, H, VW], F16)
    probs = sb("probs", [P, 2, H, P])
    p16 = sb("p16", [P, 2, 2, H, P], F16)
    pT16 = sb("pT16", [P, 2, H, P], F16)
    attn = sb("attn", [P, GT, H, HD])
    attnT = sb("attnT", [P, GT * P])
    xc = sb("xc", [P, GT, P])
    xc2 = sb("xc2", [P, GT, P])
    xs2 = sb("xs2", [P, GT, P])
    x16 = sb("x16", [P, GT, 2, P], F16)
    xT = sb("xT", [P, 2, 2, GT * P], F16)
    blank = sb("blank", [P, ROW], U32)
    bn1 = sb("bn1", [P, GT, 6])
    mv1 = sb("mv1", [P, 2, GT, 2])
    rs1 = sb("rs1", [P, 2, GT])
    bn2 = sb("bn2", [P, GT, 6])
    mv2 = sb("mv2", [P, GT, 2])
    ve1 = sb("ve1", [P, 2, GT])
    ve2 = sb("ve2", [P, GT])
    half = sb("half", [P, GT])
    rs2s = sb("rs2s", [P, GT])
    smax = sb("smax", [P, H])
    turn = sb("turn_dve", [P, 1])
    rden = sb("rden", [P, H])

    S = ps("S", [P, 4, 512])
    PT = ps("PT", [P, 2, H, P], F16)
    PV = ps("PV", [P, 512])
    M0 = ps("M0", [P, 512])
    M16 = M0[:, :].bitcast(F16).rearrange("p (a t) -> p a t", a=2)
    S_heads = S[:, :, 0:2 * P].rearrange("p r (e k) -> p r e k", e=2)
    PVh = PV[:, 0:H * VW].rearrange("p (h c) -> p h c", h=H)

    consts = sem("consts")
    prep = sem("prep")
    bias_ps = sem("bias_ps")
    loaded = [sem("loaded0"), sem("loaded1")]
    names = ["bn1_done", "aggr1", "ln1_stats", "xn_ready", "mask_ready", "bias_added", "xT_ps", "xT_sb", "q_ps", "q_sb",
             "k_ps", "k_sb", "v_ps", "v_sb", "aT_ps", "aT_sb", "out_ps", "x2_done", "bn2_done", "aggr2", "rs1_done", "rs2_done", "rows_kept", "xc1_done", "xc2_done",
             "ln2_stats", "xs2_done", "hi_done", "split_done", "x2T_ps", "x2T_sb", "lg_ps", "lg_sb",
             "s_ps", "max_done", "sub_done", "exp_done", "p_hi", "p_lo", "v_hi", "pt_ps", "pt_hi_sb", "pt_lo_sb", "pv_ps", "rec_done", "norm_done"]
    s = {n: sem(n) for n in names}

    def wait(eng, name, count):
        if not (isinstance(count, int) and count <= 0):
            eng.wait_ge(s[name], count)

    def set_up(eng, g):
        if not isinstance(g, int):
            eng.wait_ge(prep, 4)

    def has(g, off=0, n=NG):
        return not isinstance(g, int) or 0 <= g - off < n

    M0_ORDER = [("xT", -1, "xT_sb"), ("Q", -1, "q_sb"), ("K", -1, "k_sb"), ("V", -1, "v_sb"),
                ("x2T", 2, "x2T_sb"), ("aT", 1, "aT_sb"), ("lg", 2, "lg_sb"), ("out", 1, "x2_done")]

    def m0_free(pe, task, g):
        at = [t[0] for t in M0_ORDER].index(task)
        while True:
            at -= 1
            if at < 0:
                at, g = len(M0_ORDER) - 1, g - 1
                if isinstance(g, int) and g < -1:
                    return
            _, off, emptied = M0_ORDER[at]
            if has(g, off):
                wait(pe, emptied, g - off + 1)
                return

    blank_ready = sem("blank_ready")
    slots_blank = sem("slots_blank")
    xT_stored = [sem("xT_stored0"), sem("xT_stored1")]
    NCONST = 12
    nc_block = ctx.enter_context(nc.Block())

    @nc_block.sync
    def _(sp):
        for dst, src in ((ident[:], d["ident"]), (parity[:], d["parity"]), (wq[:], d["Wq"]), (wk[:], d["Wk"]),
                         (wv[:], d["Wv"]), (wo[:], d["Wo"]), (wr[:], d["Wr"]),
                         (cols[:, 0:1], d["bq"].unsqueeze(1)), (cols[:, 1:2], d["bk"].unsqueeze(1)),
                         (cols[:, 2:3], d["bv"].unsqueeze(1)),
                         (bo_rows[:], d["bo"].unsqueeze(0).to_broadcast([P, P])),
                         (no_pair[:], d["no_pair"])):
            sp.dma_start(dst, src).then_inc(consts, 16)

        def load(g, q):
            wait(sp, "mask_ready", g - 1)
            sp.dma_start(x_res[:, bass.ds(g * GT, GT), :],
                         d["x"][bass.ds(g * GT, GT)].rearrange("b t c -> t b c")).then_inc(loaded[q], 16)
            sp.dma_start(adj[:, q], d["adj"][bass.ds(g * GT, GT)].rearrange("b t c -> t b c")).then_inc(loaded[q], 16)

        def store_xT(g, q):
            wait(sp, "x2T_sb", g + 1)
            sp.dma_start(xT_dram[bass.ds(g, 1)].rearrange("o p a t -> p o a t"),
                         xT[:, q].unsqueeze(1)).then_inc(xT_stored[q], 16)

        def blank_slots(unit, n):
            sp.dma_start(slots_dram[bass.ds(unit * UT, n * UT), :].rearrange("(j p) c -> p j c", p=P),
                         blank[:].unsqueeze(1).to_broadcast([P, n * GT, ROW])).then_inc(slots_blank, 16)

        load(0, 0)
        load(1, 1)
        load(2, 0)
        load(3, 1)
        loops = NG // 2 - 2
        per_loop = NU // loops
        sp.wait_ge(blank_ready, 2)
        blank_slots(loops * per_loop, NU - loops * per_loop)
        with sp.Fori(2, NG // 2) as r:
            load(2 * r, 0)
            load(2 * r + 1, 1)
            store_xT(2 * r - 4, 0)
            store_xT(2 * r - 3, 1)
            blank_slots((r - 2) * per_loop, per_loop)
        for g in range(NG - 4, NG):
            store_xT(g, g % 2)
        sp.wait_ge(slots_blank, 16 * (loops + 1))
        sp.wait_ge(xT_stored[0], 16 * NG // 2)
        sp.wait_ge(xT_stored[1], 16 * NG // 2)

    def pair_blocks(eng, step):
        step(-1, 1)
        step(0, 0)
        step(1, 1)
        with eng.Fori(1, NG // 2 - 1) as r:
            step(2 * r, 0)
            step(2 * r + 1, 1)
        step(NG - 2, 0)
        step(NG - 1, 1)
        step(NG, 0)
        step(NG + 1, 1)

    @nc_block.gpsimd
    def _(pool):
        pool.wait_ge(consts, 16 * NCONST)
        pool.memset(ones[:], 1.0).then_inc(prep, 1)
        pool.memset(V[:, :, 1, :, :, HD:VW], 0.0)
        pool.memset(V[:, :, 0, :, :, HD:VW], VS).then_inc(prep, 1)
        pool.memset(half[:], -0.5)
        pool.memset(blank[:, 0:P], 0)
        pool.memset(blank[:, P + 1:ROW], 0).then_inc(blank_ready, 1)
        pool.tensor_copy(blank[:, P:P + 1], no_pair[:]).then_inc(blank_ready, 1)
        pool.tensor_copy(ident16[:], ident[:]).then_inc(prep, 1)
        pool.tensor_copy(identb[:], ident[:]).then_inc(prep, 1)

        def norm1(g, q):
            wait(pool, "ln1_stats", g + 1)
            wait(pool, "xT_ps", g)
            pool.tensor_tensor(rs1[:, q], ve1[:, q], half[:], ALU.pow).then_inc(s["rs1_done"], 1)
            xg = x_res[:, bass.ds(g * GT, GT), :]
            pool.wait_ge(s["rs1_done"], 1)
            pool.tensor_tensor(xc[:], xg, mv1[:, q, :, 0:1].to_broadcast([P, GT, P]),
                               ALU.subtract).then_inc(s["xc1_done"], 1)
            wait(pool, "rs1_done", g + 1)
            wait(pool, "xc1_done", g + 1)
            pool.tensor_tensor(xn[:], xc[:], rs1[:, q].unsqueeze(2).to_broadcast([P, GT, P]),
                               ALU.mult).then_inc(s["xn_ready"], 1)
            set_up(pool, g)
            wait(pool, "xn_ready", g + 1)
            if isinstance(g, int) and g == 0:
                pool.wait_ge(prep, 11)
            pool.tensor_tensor(xg, xg, out_bias[:].unsqueeze(1).to_broadcast([P, GT, P]),
                               ALU.add).then_inc(s["bias_added"], 1)

        def split(g):
            wait(pool, "ln2_stats", g + 1)
            wait(pool, "rows_kept", g)
            pool.tensor_tensor(rs2s[:], ve2[:], half[:], ALU.pow).then_inc(s["rs2_done"], 1)
            pool.tensor_tensor(xc2[:], x_res[:, bass.ds(g * GT, GT), :], mv2[:, :, 0:1].to_broadcast([P, GT, P]),
                               ALU.subtract).then_inc(s["xc2_done"], 1)
            wait(pool, "rs2_done", g + 1)
            wait(pool, "xc2_done", g + 1)
            pool.tensor_tensor(xs2[:], xc2[:], rs2s[:].unsqueeze(2).to_broadcast([P, GT, P]),
                               ALU.mult).then_inc(s["xs2_done"], 1)
            set_up(pool, g)
            wait(pool, "x2T_ps", g)
            wait(pool, "xs2_done", g + 1)
            pool.tensor_copy(x16[:, :, 0], xs2[:]).then_inc(s["hi_done"], 1)
            wait(pool, "hi_done", g + 1)
            pool.tensor_tensor(x16[:, :, 1], xs2[:], x16[:, :, 0], ALU.subtract).then_inc(s["split_done"], 1)
            set_up(pool, g)
            wait(pool, "split_done", g + 1)
            pool.tensor_copy(x_rows[:, bass.ds(g * GT, GT), :], x16[:].rearrange("p j a c -> p j (a c)"))\
                .then_inc(s["rows_kept"], 1)

        def step(g, q):
            if isinstance(g, int) and g == -1:
                norm1(0, 0)
            if has(g, 2):
                split(g - 2)
            if has(g, -2):
                norm1(g + 2, q)

        pair_blocks(pool, step)

    @nc_block.vector
    def _(dve):
        dve.wait_ge(consts, 16 * NCONST)
        dve.wait_ge(prep, 4)
        dve.tensor_scalar(wr64[:], wr[:], WS, None, ALU.mult).then_inc(prep, 1)
        dve.tensor_scalar(bv_mat[:], ones[:], cols[:, 2:3], None, ALU.mult).then_inc(prep, 1)
        dve.tensor_scalar(qb[:], cols[:, 0:1], 0.25, None, ALU.mult).then_inc(prep, 1)
        dve.tensor_scalar(kb[:], parity[:], cols[:, 1:2], None, ALU.mult).then_inc(prep, 1)
        dve.wait_ge(prep, 8)
        dve.tensor_copy(wr16[:, 0], wr64[:]).then_inc(prep, 1)
        dve.wait_ge(prep, 9)
        dve.tensor_tensor(wr16[:, 1], wr64[:], wr16[:, 0], ALU.subtract).then_inc(prep, 1)
        dve.wait_ge(bias_ps, 1)
        dve.tensor_tensor(out_bias[:], M0[:, 0:P], bo_rows[:], ALU.add).then_inc(prep, 1)

        def stats1(g, q):
            set_up(dve, g)
            dve.wait_ge(loaded[q], (g // 2 + 1) * 32 if isinstance(g, int) else (g - q) * 16 + 32)
            wait(dve, "xn_ready", g - 1)
            wait(dve, "aggr1", g)
            for j in range(GT):
                last = dve.bn_stats(bn1[:, j, :], x_res[:, g * GT + j, :])
            last.then_inc(s["bn1_done"], 1)
            wait(dve, "bn1_done", g + 1)
            if not isinstance(g, int):
                dve.memset(turn[:], 0.0)
            for j in range(GT):
                last = dve.bn_aggr(mv1[:, q, j, :], bn1[:, j, :])
            last.then_inc(s["aggr1"], 1)
            wait(dve, "aggr1", g + 1)
            dve.tensor_scalar(ve1[:, q], mv1[:, q, :, 1], EPS, None, ALU.add).then_inc(s["ln1_stats"], 1)

        def mask(g, q):
            dve.wait_ge(loaded[q], (g // 2 + 1) * 32 if isinstance(g, int) else (g - q) * 16 + 32)
            wait(dve, "s_ps", (g - 1) * GT if isinstance(g, int) else g * GT - GT)
            dve.tensor_scalar(negmask[:, q], adj[:, q], 0.0, NEG, ALU.is_le, ALU.mult).then_inc(s["mask_ready"], 1)

        def residual_and_stats2(g):
            wait(dve, "out_ps", g + 1)
            wait(dve, "bias_added", g + 1)
            xg = x_res[:, bass.ds(g * GT, GT), :]
            dve.tensor_tensor(xg, M0[:, :].rearrange("p (j c) -> p j c", j=GT), xg, ALU.add).then_inc(s["x2_done"], 1)
            set_up(dve, g)
            wait(dve, "x2_done", g + 1)
            wait(dve, "aggr2", g)
            for j in range(GT):
                last = dve.bn_stats(bn2[:, j, :], x_res[:, g * GT + j, :])
            last.then_inc(s["bn2_done"], 1)
            set_up(dve, g)
            wait(dve, "bn2_done", g + 1)
            wait(dve, "xs2_done", g)
            for j in range(GT):
                last = dve.bn_aggr(mv2[:, j, :], bn2[:, j, :])
            last.then_inc(s["aggr2"], 1)
            wait(dve, "aggr2", g + 1)
            dve.tensor_scalar(ve2[:], mv2[:, :, 1], EPS, 1.0 / (XS * XS), ALU.add, ALU.mult).then_inc(s["ln2_stats"], 1)

        def normalise(t, j):
            wait(dve, "pv_ps", t + 1)
            wait(dve, "norm_done", t)
            dve.reciprocal(rden[:], PVh[:, :, HD]).then_inc(s["rec_done"], 1)
            wait(dve, "rec_done", t + 1)
            if j == 0:
                wait(dve, "aT_ps", t // GT if isinstance(t, int) else t * 0 + t_group(t))
            dve.tensor_tensor(attn[:, j], PVh[:, :, 0:HD], rden[:].unsqueeze(2).to_broadcast([P, H, HD]),
                              ALU.mult).then_inc(s["norm_done"], 1)

        group_now = [0]

        def t_group(t):
            return group_now[0]

        def softmax_shift(t, b):
            wait(dve, "s_ps", t + 1)
            wait(dve, "sub_done", t)
            dve.tensor_reduce(smax[:].rearrange("p (r e) -> p r e", e=2), S_heads, AX_X, ALU.max).then_inc(s["max_done"], 1)
            wait(dve, "max_done", t + 1)
            wait(dve, "p_lo", t - 1)
            dve.tensor_tensor(probs[:, b].rearrange("p (r e) k -> p r e k", e=2), S_heads,
                              smax[:].rearrange("p (r e) -> p r e", e=2).unsqueeze(3).to_broadcast([P, 4, 2, P]),
                              ALU.subtract).then_inc(s["sub_done"], 1)

        def low_probs(t, b):
            wait(dve, "p_hi", t + 1)
            dve.scalar_tensor_tensor(out=p16[:, b, 1], in0=probs[:, b], scalar=PS, in1=p16[:, b, 0],
                                     op0=ALU.mult, op1=ALU.subtract).then_inc(s["p_lo"], 1)

        def keep_low_transposed(t):
            wait(dve, "pt_ps", t + 1)
            wait(dve, "pv_ps", t)
            dve.tensor_copy(pT16[:, 1], PT[:, 1]).then_inc(s["pt_lo_sb"], 1)

        def low_values(g, q):
            wait(dve, "v_hi", g + 1)
            dve.scalar_tensor_tensor(out=V[:, q, 1, :, :, 0:HD].rearrange("p j h c -> p (j h) c"),
                                     in0=M0[:, :].rearrange("p (j c) -> p j c", c=HD), scalar=VS,
                                     in1=V[:, q, 0, :, :, 0:HD].rearrange("p j h c -> p (j h) c"),
                                     op0=ALU.mult, op1=ALU.subtract).then_inc(s["v_sb"], 1)

        def step(g, q):
            if isinstance(g, int) and g == -1:
                stats1(0, 0)
                mask(0, 0)
                stats1(1, 1)
                low_values(0, 0)
                return
            for j in range(GT):
                t = g * GT + j
                if has(t, 3, NT):
                    group_now[0] = g if j == 3 else g - 1
                    normalise(t - 3, (j - 3) % GT)
                if j == 0 and has(g, 2):
                    residual_and_stats2(g - 2)
                if j == 1 and has(g, -2):
                    stats1(g + 2, q)
                if j == 2 and has(g, -1):
                    mask(g + 1, 1 - q)
                if has(t, 1, NT):
                    low_probs(t - 1, (j - 1) % 2)
                if j == 2 and has(g, -1):
                    low_values(g + 1, 1 - q)
                if has(t, 0, NT):
                    softmax_shift(t, j % 2)
                if has(t, 1, NT):
                    keep_low_transposed(t - 1)

        pair_blocks(dve, step)

    @nc_block.scalar
    def _(act):
        act.wait_ge(prep, 8)

        def evac(task, g, q):
            if task == "xT":
                wait(act, "xT_ps", g + 1)
                act.activation(xnT[:], M0[:, :], ACT.Copy).then_inc(s["xT_sb"], 1)
            elif task == "Q":
                wait(act, "q_ps", g + 1)
                act.activation(QT[:, q], M0[:, :], ACT.Identity, bias=qb[:], scale=0.25).then_inc(s["q_sb"], 1)
            elif task == "K":
                wait(act, "k_ps", g + 1)
                act.activation(KT[:, q, 0], M0[:, :], ACT.Identity, bias=kb[:, 0:1], scale=parity[:, 0:1])
                act.activation(KT[:, q, 1], M0[:, :], ACT.Identity, bias=kb[:, 1:2],
                               scale=parity[:, 1:2]).then_inc(s["k_sb"], 1)
            elif task == "V":
                wait(act, "v_ps", g + 1)
                act.activation(V[:, q, 0, :, :, 0:HD].rearrange("p j h c -> p (j h) c"),
                               M0[:, :].rearrange("p (j c) -> p j c", c=HD), ACT.Copy, scale=VS).then_inc(s["v_hi"], 1)
            elif task == "aT":
                wait(act, "aT_ps", g + 1)
                act.activation(attnT[:], M0[:, :], ACT.Copy).then_inc(s["aT_sb"], 1)
            elif task == "x2T":
                wait(act, "x2T_ps", g + 1)
                if not isinstance(g, int) or g >= 2:
                    act.wait_ge(xT_stored[q], g * 8 if q == 0 else (g - 1) * 8)
                act.activation(xT[:, q], M16, ACT.Copy).then_inc(s["x2T_sb"], 1)
            elif task == "lg":
                set_up(act, g)
                wait(act, "lg_ps", g + 1)
                act.activation(logits[:, bass.ds(g * GT, GT), :], M0[:, 0:GT * E].rearrange("p (j e) -> p j e", e=E),
                               ACT.Copy, scale=1.0 / (XS * WS)).then_inc(s["lg_sb"], 1)

        def slot_tasks(g, q, j):
            a, b = {0: (("xT", g + 1, 1 - q), ("Q", g + 1, 1 - q)), 1: (("K", g + 1, 1 - q), ("V", g + 1, 1 - q)),
                    2: (("x2T", g - 2, q), ("aT", g - 1, 1 - q)), 3: (("lg", g - 2, q), None)}[j]
            return a, b

        def step(g, q):
            for j in range(GT):
                t = g * GT + j
                a = slot_tasks(g, q, j)[0]
                b = slot_tasks(g, q, j - 1)[1] if j else None
                if has(t, 1, NT):
                    wait(act, "sub_done", t)
                    pr = probs[:, (j - 1) % 2]
                    act.activation(pr, pr, ACT.Exp).then_inc(s["exp_done"], 1)
                    wait(act, "exp_done", t)
                    wait(act, "pt_ps", t - 2)
                    act.activation(p16[:, (j - 1) % 2, 0], pr, ACT.Copy, scale=PS).then_inc(s["p_hi"], 1)
                if b and has(b[1]):
                    evac(*b)
                if has(a[1]):
                    evac(*a)
                if has(t, 1, NT):
                    wait(act, "pt_ps", t)
                    wait(act, "pv_ps", t - 1)
                    act.activation(pT16[:, 0], PT[:, 0], ACT.Copy).then_inc(s["pt_hi_sb"], 1)

        pair_blocks(act, step)

    @nc_block.tensor
    def _(pe):
        pe.wait_ge(prep, 8)
        pe.matmul(M0[:, 0:P], bv_mat[:], wo[:], start=True, stop=True).then_inc(bias_ps, 1)
        pe.wait_ge(prep, 11)

        def m0_task(task, g, q, step_g):
            if task == "xT":
                wait(pe, "xn_ready", g + 1)
                m0_free(pe, task, step_g)
                for j in range(GT):
                    mm = pe.transpose(M0[:, j * P:(j + 1) * P], xn[:, j], ident[:])
                mm.then_inc(s["xT_ps"], 1)
            elif task in "QK":
                m0_free(pe, task, step_g)
                mm = pe.matmul(M0[:, :], (wq if task == "Q" else wk)[:], xnT[:], start=True, stop=True)
                mm.then_inc(s["q_ps" if task == "Q" else "k_ps"], 1)
            elif task == "V":
                m0_free(pe, task, step_g)
                for j in range(GT):
                    mm = pe.matmul(M0[:, j * P:(j + 1) * P], xnT[:, j * P:(j + 1) * P], wv[:], start=True, stop=True)
                mm.then_inc(s["v_ps"], 1)
            elif task == "aT":
                wait(pe, "norm_done", (g + 1) * GT)
                m0_free(pe, task, step_g)
                for j in range(GT):
                    mm = pe.transpose(M0[:, j * P:(j + 1) * P], attn[:, j].rearrange("p h c -> p (h c)"), ident[:])
                mm.then_inc(s["aT_ps"], 1)
            elif task == "out":
                wait(pe, "aT_sb", g + 1)
                m0_free(pe, task, step_g)
                for j in range(GT):
                    mm = pe.matmul(M0[:, j * P:(j + 1) * P], attnT[:, j * P:(j + 1) * P], wo[:], start=True, stop=True)
                mm.then_inc(s["out_ps"], 1)
            elif task == "x2T":
                wait(pe, "split_done", g + 1)
                m0_free(pe, task, step_g)
                for part in range(2):
                    for j in range(GT):
                        mm = pe.transpose(M16[:, part, j * P:(j + 1) * P], x16[:, j, part], ident16[:])
                mm.then_inc(s["x2T_ps"], 1)
            elif task == "lg":
                wait(pe, "x2T_sb", g + 1)
                m0_free(pe, task, step_g)
                for j in range(GT):
                    for n, (a, b) in enumerate(((0, 0), (0, 1), (1, 0))):
                        mm = pe.matmul(M0[:, j * E:(j + 1) * E], xT[:, q, a, j * P:(j + 1) * P],
                                       wr16[:, b], start=n == 0, stop=n == 2)
                mm.then_inc(s["lg_ps"], 1)

        def step(g, q):
            for j in range(GT):
                t = g * GT + j
                tasks = {0: (("xT", g + 1, 1 - q), ("Q", g + 1, 1 - q)), 1: (("K", g + 1, 1 - q), ("V", g + 1, 1 - q)),
                         2: (("x2T", g - 2, q), ("aT", g - 1, 1 - q)), 3: (("lg", g - 2, q), ("out", g - 1, 1 - q))}[j]
                if has(t, 0, NT):
                    if j == 0:
                        wait(pe, "k_sb", g + 1)
                        wait(pe, "mask_ready", g + 1)
                    wait(pe, "sub_done", t)
                    for r in range(4):
                        rows = slice(32 * r, 32 * r + 32)
                        pe.matmul(S_heads[:, r], QT[rows, q, j * P:(j + 1) * P], KT[rows, q, :, j * P:(j + 1) * P],
                                  start=True, stop=False)
                    for r in range(4):
                        mm = pe.matmul(S_heads[:, r], identb[:], negmask[:, q, j].unsqueeze(1).to_broadcast([P, 2, P]),
                                       start=False, stop=True)
                    mm.then_inc(s["s_ps"], 1)
                if has(t, 2, NT):
                    vq, vj = (q, j - 2) if j >= 2 else (1 - q, j + 2)
                    if vj == 0:
                        wait(pe, "v_sb", g + 1)
                    wait(pe, "pt_hi_sb", t - 1)
                    wait(pe, "pt_lo_sb", t - 1)
                    wait(pe, "norm_done", t - 2)
                    for h in range(H):
                        for n, (a, b) in enumerate(((0, 0), (0, 1), (1, 0))):
                            mm = pe.matmul(PVh[:, h], pT16[:, a, h], V[:, vq, b, vj, h], start=n == 0, stop=n == 2)
                    mm.then_inc(s["pv_ps"], 1)
                if has(tasks[0][1]):
                    m0_task(*tasks[0], g)
                if has(t, 1, NT):
                    wait(pe, "p_lo", t)
                    wait(pe, "pt_hi_sb", t - 1)
                    wait(pe, "pt_lo_sb", t - 1)
                    for part in range(2):
                        for h in range(H):
                            mm = pe.transpose(PT[:, part, h], p16[:, (j - 1) % 2, part, h], ident16[:])
                    mm.then_inc(s["pt_ps"], 1)
                if has(tasks[1][1]):
                    m0_task(*tasks[1], g)

        pair_blocks(pe, step)


def router_phase(nc, ctx, d, f, logits, mask, pair_weight, pair_slot, unit_expert):
    def sb(name, shape, dt=F32):
        return ctx.enter_context(nc.sbuf_tensor(name, shape, dt))

    def sem(name):
        return ctx.enter_context(nc.semaphore(name))

    rank_key = sb("rank_key", [P, E])
    before = sb("before", [P, P])
    all_ones = sb("all_ones", [P, P])
    unit_ids = sb("unit_ids", [1, NU])
    pick1 = sb("pick1", [P, NT, E])
    pick2 = sb("pick2", [P, NT, E])
    rest = sb("rest", [P, NT, E])
    eq = sb("eq", [P, NT, E])
    run_a = rest
    run_b = logits
    m1, m2, key, diff, e2, den, slot_f = (sb(f"rt_{n}", [P, NT]) for n in "abcdefg")
    need = sb("need", [P, E])
    need_i = sb("need_i", [P, E], I32)
    first = sb("first", [P, E])
    last = sb("last", [P, E])
    offset = sb("offset", [P, E])
    passed = sb("passed", [1, NU, E])
    expert_f = sb("expert_f", [1, NU])
    totals = f.B7[:, 0:2 * E].rearrange("p (a e) -> p a e", a=2)
    w_loaded = [sem(f"w_loaded{i}") for i in range(FC)]
    w_scaled, w_hi, w_split = sem("w_scaled"), sem("w_hi"), sem("w_split")
    loaded, diff_ready, exp2_ready = sem("rt_loaded"), sem("diff_ready"), sem("exp2_ready")
    routed, counts_ready, totals_ready = sem("routed"), sem("counts_ready"), sem("totals_ready")
    block = ctx.enter_context(nc.Block())

    w_src = [d["W1p"][e] for e in range(E)] + [d["W1s"]] + \
            [d["W2p"][e].rearrange("(c p) d -> p c d", p=P) for e in range(E)] + \
            [d["W2s"].rearrange("(c p) d -> p c d", p=P)]

    def w_parts(n):
        return [f.w1[:, k, n] if n < EA else f.w2[:, k, n - EA].rearrange("p c d -> p (c d)") for k in range(2)]

    def wide(v):
        return v.unsqueeze(2).to_broadcast([P, NT, E])

    def over_tiles(v):
        return v.unsqueeze(1).to_broadcast([P, NT, E])

    @block.sync
    def _(sp):
        sp.dma_start(rank_key[:], d["rank_key"].unsqueeze(0).to_broadcast([P, E])).then_inc(loaded, 16)
        sp.dma_start(before[:], d["before"]).then_inc(loaded, 16)
        sp.dma_start(unit_ids[:], d["unit-ids"].unsqueeze(0)).then_inc(loaded, 16)
        for n, src in enumerate(w_src):
            if n >= FC:
                sp.wait_ge(w_split, n - FC + 1)
            st = f.hid[:, n % FC]
            dst = st if n < EA else st.rearrange("p (c d) -> p c d", c=FC)
            sp.dma_start(dst, src).then_inc(w_loaded[n % FC], 16)


    @block.scalar
    def _(act):
        for n in range(len(w_src)):
            st = f.hid[:, n % FC]
            act.wait_ge(w_loaded[n % FC], 16 * (n // FC + 1))
            act.activation(st, st, ACT.Copy, scale=WS).then_inc(w_scaled, 1)
            act.wait_ge(w_scaled, n + 1)
            act.activation(w_parts(n)[0], st, ACT.Copy).then_inc(w_hi, 1)
            if n == EA:
                act.wait_ge(diff_ready, 1)
                act.activation(e2[:], diff[:], ACT.Exp).then_inc(exp2_ready, 1)

    @block.gpsimd
    def _(pool):
        for n in range(len(w_src)):
            pool.wait_ge(w_hi, n + 1)
            pool.tensor_tensor(w_parts(n)[1], f.hid[:, n % FC], w_parts(n)[0], ALU.subtract).then_inc(w_split, 1)

    @block.tensor
    def _(pe):
        pe.wait_ge(counts_ready, 1)
        pe.matmul(totals[:, 0], before[:], run_b[:, NT - 1, :], start=True, stop=True)
        pe.matmul(totals[:, 1], all_ones[:], run_b[:, NT - 1, :], start=True, stop=True).then_inc(totals_ready, 1)

    @block.vector
    def _(dve):
        steps = [0]

        def then(ins):
            steps[0] += 1
            ins.then_inc(routed, 1)
            dve.wait_ge(routed, steps[0])

        keys = over_tiles(rank_key[:])
        dve.wait_ge(loaded, 48)
        dve.memset(all_ones[:], 1.0)
        for src, top, pick in ((logits, m1, pick1), (rest, m2, pick2)):
            then(dve.tensor_reduce(top[:], src[:], AX_X, ALU.max))
            then(dve.tensor_tensor(eq[:], src[:], wide(top[:]), ALU.is_equal))
            then(dve.tensor_tensor(eq[:], eq[:], keys, ALU.mult))
            then(dve.tensor_reduce(key[:], eq[:], AX_X, ALU.max))
            then(dve.tensor_tensor(pick[:], wide(key[:]), keys, ALU.is_equal))
            if pick is pick1:
                then(dve.scalar_tensor_tensor(out=rest[:], in0=pick1[:], scalar=-3.0e38, in1=logits[:],
                                              op0=ALU.mult, op1=ALU.add))
        dve.tensor_tensor(diff[:], m2[:], m1[:], ALU.subtract).then_inc(diff_ready, 1)

        then(dve.tensor_tensor(run_b[:], pick1[:], pick2[:], ALU.add))
        src, dst, n = run_b, run_a, 1
        while n < NT:
            dve.tensor_copy(dst[:, 0:n], src[:, 0:n])
            then(dve.tensor_tensor(dst[:, n:NT], src[:, n:NT], src[:, 0:NT - n], ALU.add))
            src, dst, n = dst, src, 2 * n
        if src is not run_b:
            then(dve.tensor_copy(run_b[:], src[:]))
        dve.tensor_copy(eq[:, 0], run_b[:, NT - 1]).then_inc(counts_ready, 1)
        dve.wait_ge(totals_ready, 1)
        then(dve.tensor_scalar(need[:], totals[:, 1], float(UT - 1), None, ALU.add))
        then(dve.tensor_copy(need_i[:], need[:]))
        then(dve.tensor_scalar(need_i[:], need_i[:], UT.bit_length() - 1, None, ALU.logical_shift_right))
        then(dve.tensor_copy(need[:], need_i[:]))
        then(dve.memset(first[:, 0:1], 0.0))
        for e in range(1, E):
            then(dve.tensor_tensor(first[:, e:e + 1], first[:, e - 1:e], need[:, e - 1:e], ALU.add))
        then(dve.tensor_tensor(last[:], first[:], need[:], ALU.add))
        then(dve.tensor_scalar(offset[:], first[:], float(UT), -1.0, ALU.mult, ALU.add))
        then(dve.tensor_tensor(offset[:], totals[:, 0], offset[:], ALU.add))
        then(dve.tensor_tensor(run_b[:], run_b[:], over_tiles(offset[:]), ALU.add))
        for k, pick in enumerate((pick1, pick2)):
            then(dve.tensor_tensor(eq[:], pick[:], run_b[:], ALU.mult))
            then(dve.tensor_reduce(slot_f[:], eq[:], AX_X, ALU.add))
            then(dve.tensor_copy(pair_slot[:, :, k], slot_f[:]))
        then(dve.tensor_tensor(passed[:], last[0:1].unsqueeze(1).to_broadcast([1, NU, E]),
                               unit_ids[:].unsqueeze(2).to_broadcast([1, NU, E]), ALU.is_le))
        then(dve.tensor_reduce(expert_f[:], passed[:], AX_X, ALU.add))
        then(dve.tensor_scalar(expert_f[:], expert_f[:], float(E - 1), None, ALU.min))
        then(dve.tensor_copy(unit_expert[:], expert_f[:]))

        dve.wait_ge(exp2_ready, 1)
        then(dve.tensor_scalar(den[:], e2[:], 1.0, None, ALU.add))
        then(dve.reciprocal(pair_weight[:, :, 0], den[:]))
        then(dve.tensor_tensor(pair_weight[:, :, 1], e2[:], pair_weight[:, :, 0], ALU.mult))
        then(dve.tensor_tensor(pick1[:], pick1[:], wide(pair_weight[:, :, 0]), ALU.mult))
        then(dve.tensor_tensor(pick2[:], pick2[:], wide(pair_weight[:, :, 1]), ALU.mult))
        then(dve.tensor_tensor(mask[:, :, 0:E], pick1[:], pick2[:], ALU.add))
        then(dve.memset(mask[:, :, E:EA], 1.0))


class Ffn:

    def __init__(self, nc, ctx):
        def ps(name, shape, dt=F32):
            return ctx.enter_context(nc.psum_tensor(name, shape, dt))

        def sb(name, shape, dt=F32):
            return ctx.enter_context(nc.sbuf_tensor(name, shape, dt))

        self.w1 = sb("w1", [P, 2, EA, F], F16)
        self.w2 = sb("w2", [P, 2, EA, FC, P], F16)
        self.b1 = sb("b1", [P, EA, FC])
        self.hid = sb("hid", [P, FC, F])
        self.Z = ps("Z", [P, FC, UT])
        self.Y = ps("Y", [P, 2, GT, P])
        self.B6 = ps("B6", [P, 512])
        self.B7 = ps("B7", [P, 512])

    def unit_buffers(self, nc, ctx):
        def sb(name, shape, dt=F32):
            return ctx.enter_context(nc.sbuf_tensor(name, shape, dt))

        self.turn = sb("turn", [P, 1])
        self.turn_pool = sb("turn_pool", [P, 2])
        self.h16 = sb("h16", [P, 2, 2, FC, F], F16)
        self.xT = sb("xTu", [P, 2, 2, UT], F16)

    def semaphores(self, nc, ctx, kind):
        def sem(name):
            return ctx.enter_context(nc.semaphore(f"{name}_{kind}"))

        self.xT_ready = [sem("xT_ready0"), sem("xT_ready1")]
        self.z_ps, self.gelu_done, self.hi_done, self.lo_done = sem("z_ps"), sem("gelu"), sem("hhi"), sem("hlo")
        self.y_ps, self.y_read, self.took_wait = sem("y_ps"), sem("y_read"), sem("took_wait")

    def take_wait(self, pool, n):
        if not (isinstance(n, int) and n == 0):
            pool.wait_ge(self.took_wait, n)
        pool.tensor_tensor(self.turn_pool[:, 0:1], self.turn_pool[:, 1:2], self.turn_pool[:, 1:2],
                           ALU.add).then_inc(self.took_wait, 1)

    def hidden(self, pe, u, e, b):
        for c in range(FC):
            if not (isinstance(u, int) and u == 0):
                pe.wait_ge(self.gelu_done, u * FC + (c + 1 - FC))
            for n, (k, m) in enumerate(((0, 0), (0, 1), (1, 0))):
                mm = pe.matmul(self.Z[:, c], self.w1[:, k, :, c * P:(c + 1) * P][:, e, :], self.xT[:, b, m],
                               start=n == 0, stop=n == 2)
            mm.then_inc(self.z_ps, 1)

    def output(self, pe, u, e, b):
        pe.wait_ge(self.lo_done, u * FC + FC)
        if not (isinstance(u, int) and u < 2):
            pe.wait_ge(self.y_read, u - 1)
        for j in range(GT):
            for c in range(FC):
                for n, (k, m) in enumerate(((0, 0), (0, 1), (1, 0))):
                    mm = pe.matmul(self.Y[:, b, j], self.h16[:, b, k, c, j * P:(j + 1) * P], self.w2[:, m, e, c],
                                   start=c == 0 and n == 0, stop=c == FC - 1 and n == 2)
        mm.then_inc(self.y_ps, 1)

    def activate(self, act, u, e, b):
        def hi(c):
            act.wait_ge(self.gelu_done, u * FC + c + 1)
            if c == 0 and not (isinstance(u, int) and u < 2):
                act.wait_ge(self.y_ps, u - 1)
            act.activation(self.h16[:, b, 0, c], self.hid[:, c], ACT.Copy, scale=HS).then_inc(self.hi_done, 1)

        for c in range(FC):
            act.wait_ge(self.z_ps, u * FC + c + 1)
            if not (isinstance(u, int) and u == 0):
                act.wait_ge(self.lo_done, u * FC + (c + 1 - FC))
            if c:
                hi(c - 1)
            else:
                act.activation(self.turn[:], self.b1[:, 0, 0:1], ACT.Copy)
            act.activation(self.hid[:, c], self.Z[:, c], ACT.Gelu, bias=self.b1[:, e, c:c + 1],
                           scale=1.0 / (XS * WS)).then_inc(self.gelu_done, 1)
        hi(FC - 1)

    def lows(self, dve, u, b, after=None):
        for c in range(FC):
            dve.wait_ge(self.hi_done, u * FC + c + 1)
            dve.scalar_tensor_tensor(out=self.h16[:, b, 1, c], in0=self.hid[:, c], scalar=HS,
                                     in1=self.h16[:, b, 0, c], op0=ALU.mult, op1=ALU.subtract).then_inc(self.lo_done, 1)
            if after:
                after(c)


def shared_phase(nc, ctx, d, f, x_res, x_rows, mask, pair_slot, xT_dram, slots_dram):
    def sb(name, shape, dt=F32):
        return ctx.enter_context(nc.sbuf_tensor(name, shape, dt))

    def sem(name):
        return ctx.enter_context(nc.semaphore(name))

    rows = sb("rows", [P, TOP * GT, ROW], U32)
    row_slot = sb("row_slot", [P, TOP * GT], U32)
    pair_ids = sb("pair_ids", [P, NT, TOP], U32)
    identc = sb("identc", [P, P])
    b1_rows = sb("b1_rows", [EA * FC, P])
    b2 = sb("b2", [EA, P])
    mask_u = sb("mask_u", [P, GT, EA])
    maskT = sb("maskT", [EA, UT])
    f.semaphores(nc, ctx, "s")
    c_loaded = sem("c_loaded")
    b1_ps, b1_sb = sem("b1_ps"), sem("b1_sb")
    mask_copied, mt_ps, mt_sb, bias_ps, bias_done = (sem(n) for n in ("mask_copied", "mt_ps", "mt_sb", "bi_ps", "bi_done"))
    rows_ready = sem("rows_ready")
    turn_set = sem("turn_set")
    row_sent = [sem(f"row_sent{i}") for i in range(TOP * GT)]
    block = ctx.enter_context(nc.Block())
    U = NG

    @block.sync
    def _(sp):
        sp.dma_start(identc[:], d["ident"]).then_inc(c_loaded, 16)
        sp.dma_start(b1_rows[0:E * FC], d["b1p"].rearrange("e (c p) -> (e c) p", p=P)).then_inc(c_loaded, 16)
        sp.dma_start(b1_rows[E * FC:EA * FC], d["b1s"].rearrange("(c p) -> c p", p=P)).then_inc(c_loaded, 16)
        sp.dma_start(b2[0:E], d["b2p"]).then_inc(c_loaded, 16)
        sp.dma_start(b2[E:EA], d["b2s"].unsqueeze(0)).then_inc(c_loaded, 16)
        sp.dma_start(pair_ids[:], d["pair-ids"]).then_inc(c_loaded, 16)
        def load(u, b):
            if not (isinstance(u, int) and u < 2):
                sp.wait_ge(f.z_ps, u * FC - FC)
            sp.dma_start(f.xT[:, b].unsqueeze(1), xT_dram[bass.ds(u, 1)].rearrange("o p a t -> p o a t"))\
                .then_inc(f.xT_ready[b], 16)

        load(0, 0)
        load(1, 1)
        with sp.Fori(1, U // 2) as r:
            load(2 * r, 0)
            load(2 * r + 1, 1)

    @block.gpsimd
    def _(pool):
        def send(u):
            for n in range(TOP * GT):
                if n % TOP == 0:
                    pool.wait_ge(rows_ready, u * GT + n // TOP + 1)
                    f.take_wait(pool, u * GT + n // TOP)
                pool.indirect_dma_start(slots_dram, bass.IndirectOffsetOnAxis(ap=row_slot[:, n:n + 1], axis=0),
                                        rows[:, n], None).then_inc(row_sent[n], 16)

        pool.memset(f.turn_pool[:], 0.0).then_inc(turn_set, 1)
        pool.wait_ge(turn_set, 1)
        send(0)
        with pool.Fori(1, U) as u:
            send(u)
        for n in range(TOP * GT):
            pool.wait_ge(row_sent[n], 16 * U)

    @block.tensor
    def _(pe):
        pe.wait_ge(c_loaded, 16 * 6)
        pe.transpose(f.B6[:, 0:EA * FC], b1_rows[:], identc[0:EA * FC, 0:EA * FC]).then_inc(b1_ps, 1)
        pe.wait_ge(b1_sb, 1)

        def unit(u, b):
            pe.wait_ge(mask_copied, u + 1)
            if not (isinstance(u, int) and u == 0):
                pe.wait_ge(mt_sb, u)
            for j in range(GT):
                mm = pe.transpose(f.B6[0:EA, j * P:(j + 1) * P], mask_u[:, j], identc[:])
            mm.then_inc(mt_ps, 1)
            pe.wait_ge(f.xT_ready[b], u * 8 + 16 if b == 0 else u * 8 + 8)
            f.hidden(pe, u, SHARED, b)
            pe.wait_ge(mt_sb, u + 1)
            if not (isinstance(u, int) and u == 0):
                pe.wait_ge(bias_done, u)
            for j in range(GT):
                mm = pe.matmul(f.B7[:, j * P:(j + 1) * P], maskT[:, j * P:(j + 1) * P], b2[:], start=True, stop=True)
            mm.then_inc(bias_ps, 1)
            if not (isinstance(u, int) and u == 0):
                f.output(pe, u - 1, SHARED, 1 - b)

        unit(0, 0)
        unit(1, 1)
        unit(2, 0)
        unit(3, 1)
        with pe.Fori(2, U // 2) as r:
            unit(2 * r, 0)
            unit(2 * r + 1, 1)
        f.output(pe, U - 1, SHARED, 1)

    @block.scalar
    def _(act):
        act.wait_ge(b1_ps, 1)
        act.activation(f.b1[:].rearrange("p e c -> p (e c)"), f.B6[:, 0:EA * FC], ACT.Copy).then_inc(b1_sb, 1)

        def unit(u, b):
            act.wait_ge(mt_ps, u + 1)
            if not (isinstance(u, int) and u == 0):
                act.wait_ge(bias_ps, u)
            act.activation(maskT[:], f.B6[0:EA, :], ACT.Copy).then_inc(mt_sb, 1)
            f.activate(act, u, SHARED, b)

        unit(0, 0)
        unit(1, 1)
        with act.Fori(1, U // 2) as r:
            unit(2 * r, 0)
            unit(2 * r + 1, 1)

    @block.vector
    def _(dve):
        dve.wait_ge(c_loaded, 16 * 6)
        def copy(dst, src):
            return dve.tensor_scalar(dst, src, 1.0, None, ALU.mult)

        def stage_rows(u, j):
            for k in range(TOP):
                n = j * TOP + k
                if not (isinstance(u, int) and u == 0):
                    dve.wait_ge(row_sent[n], u * 16)
                t = bass.ds(u * GT + j, 1)
                copy(rows[:, n:n + 1, 0:P].bitcast(F16), x_rows[:, t, :])
                copy(rows[:, n, P:P + 1], pair_ids[:, t, k])
                ins = copy(row_slot[:, n:n + 1], pair_slot[:, t, k])
            ins.then_inc(rows_ready, 1)

        def mask_copy(u):
            if not (isinstance(u, int) and u == 0):
                dve.wait_ge(mt_ps, u)
            copy(mask_u[:], mask[:, bass.ds(u * GT, GT), :]).then_inc(mask_copied, 1)

        def bias_add(u):
            dve.wait_ge(bias_ps, u + 1)
            xg = x_res[:, bass.ds(u * GT, GT), :]
            dve.tensor_tensor(xg, f.B7[:, :].rearrange("p (j c) -> p j c", j=GT), xg, ALU.add).then_inc(bias_done, 1)

        def add(u, b):
            dve.wait_ge(f.y_ps, u + 1)
            dve.wait_ge(bias_done, u + 1)
            xg = x_res[:, bass.ds(u * GT, GT), :].rearrange("p j c -> p (j c)")
            dve.scalar_tensor_tensor(out=xg, in0=f.Y[:, b].rearrange("p j c -> p (j c)"), scalar=1.0 / (HS * WS),
                                     in1=xg, op0=ALU.mult, op1=ALU.add).then_inc(f.y_read, 1)

        def unit(u, b):
            mask_copy(u)
            f.lows(dve, u, b, after=lambda c: stage_rows(u, c))
            bias_add(u)
            if not (isinstance(u, int) and u == 0):
                add(u - 1, 1 - b)

        dve.memset(rows[:, :, P + 1:ROW], 0)
        unit(0, 0)
        unit(1, 1)
        with dve.Fori(1, U // 2) as r:
            unit(2 * r, 0)
            unit(2 * r + 1, 1)
        add(U - 1, 1)


def routed_phase(nc, ctx, d, f, x_rows, unit_expert, slots_dram, pairs_dram):
    def sem(name):
        return ctx.enter_context(nc.semaphore(name))

    f.semaphores(nc, ctx, "r")
    spare = x_rows[:, :, :].rearrange("p t c -> p (t c)")
    NIN = 4
    slot_rows = [spare[:, 2 * n * GT * ROW:2 * (n + 1) * GT * ROW].bitcast(U32).rearrange("p (j c) -> p j c", c=ROW)
                 for n in range(NIN)]
    at = 2 * NIN * GT * ROW
    y_sb = [spare[:, at + n * 2 * UT:at + (n + 1) * 2 * UT].bitcast(F32).rearrange("p (j c) -> p j c", c=P)
            for n in range(NIN)]
    at += NIN * 2 * UT
    ident16 = spare[:, at:at + P]
    at += P
    pair_of = [spare[:, at + n * 2 * GT:at + (n + 1) * 2 * GT].bitcast(U32) for n in range(NIN)]
    numbers_kept = sem("numbers_kept")
    loaded = [sem(f"slots_in{n}") for n in range(NIN)]
    sent = [sem(f"y_sent{n}") for n in range(NIN)]
    id_loaded, id_ready, t_ps, t_sb = sem("id_loaded"), sem("id_ready"), sem("t_ps"), sem("t_sb")
    block = ctx.enter_context(nc.Block())
    U = NU
    T16 = f.B6[:, :].bitcast(F16).rearrange("p (a t) -> p a t", a=2)

    def quads(eng, unit):
        for u in range(NIN):
            unit(u, u)
        with eng.Fori(1, U // NIN - 1) as r:
            for n in range(NIN):
                unit(NIN * r + n, n)
        for n in range(NIN):
            unit(U - NIN + n, n)

    def turns(u, n):
        return (u - n) * (16 // NIN)

    def early(u, n=0):
        return isinstance(u, int) and u < n

    @block.sync
    def _(sp):
        sp.dma_start(f.hid[:, 0, 0:P], d["ident"]).then_inc(id_loaded, 16)

        def load(u, n):
            if not early(u, NIN):
                sp.wait_ge(numbers_kept, u + 1 - NIN)
            sp.dma_start(slot_rows[n], slots_dram[bass.ds(u * UT, UT), :].rearrange("(j p) c -> p j c", p=P))\
                .then_inc(loaded[n], 16)

        quads(sp, load)

    @block.gpsimd
    def _(pool):
        def send(u, n):
            pool.wait_ge(f.y_read, u + 1)
            f.take_wait(pool, u)
            for j in range(GT):
                pool.indirect_dma_start(
                    pairs_dram,
                    bass.IndirectOffsetOnAxis(ap=pair_of[n][:, j:j + 1], axis=0),
                    y_sb[n][:, j], None,
                    bounds_check=TOP * NT * P - 1, oob_is_err=False).then_inc(sent[n], 16)

        quads(pool, send)
        for n in range(NIN):
            pool.wait_ge(sent[n], 16 * GT * U // NIN)

    @block.tensor
    def _(pe):
        pe.wait_ge(id_ready, 1)
        experts = {}

        def turn(u, n):
            pe.wait_ge(loaded[n], turns(u, n) + 16)
            if not early(u, 1):
                pe.wait_ge(t_sb, u)
            for part in range(2):
                for j in range(GT):
                    mm = pe.transpose(T16[:, part, j * P:(j + 1) * P], slot_rows[n][:, j, part * P // 2:(part + 1) * P // 2].bitcast(F16),
                                      ident16)
            mm.then_inc(t_ps, 1)

        def expert(u):
            return pe.value_load(unit_expert[0:1, bass.ds(u, 1)], min_val=0, max_val=E - 1)

        turn(0, 0)

        def unit(u, n):
            if not (isinstance(u, int) and u == U - 1):
                turn(u + 1, (n + 1) % NIN)
            pe.wait_ge(t_sb, u + 1)
            f.hidden(pe, u, expert(u), n % 2)
            if not early(u, 1):
                f.output(pe, u - 1, expert(u - 1), 1 - n % 2)

        quads(pe, unit)
        f.output(pe, U - 1, expert(U - 1), 1)

    @block.scalar
    def _(act):
        def unit(u, n):
            e = act.value_load(unit_expert[0:1, bass.ds(u, 1)], min_val=0, max_val=E - 1)
            f.activate(act, u, e, n % 2)

        quads(act, unit)

    @block.vector
    def _(dve):
        dve.wait_ge(id_loaded, 16)
        dve.tensor_copy(ident16, f.hid[:, 0, 0:P]).then_inc(id_ready, 1)
        dve.wait_ge(id_ready, 1)

        def keep_xT(u, n):
            dve.wait_ge(t_ps, u + 1)
            if not early(u, 2):
                dve.wait_ge(f.z_ps, u * FC - FC)
            dve.tensor_copy(f.xT[:, n % 2], T16).then_inc(t_sb, 1)

        def keep_y(u, n):
            dve.wait_ge(f.y_ps, u + 1)
            if not early(u, NIN):
                dve.wait_ge(sent[n], turns(u, n) * GT)
            dve.tensor_scalar(y_sb[n], f.Y[:, n % 2], 1.0 / (HS * WS), None, ALU.mult).then_inc(f.y_read, 1)

        def keep_numbers(u, n):
            dve.wait_ge(t_sb, u + 1)
            if not early(u, NIN):
                dve.wait_ge(sent[n], turns(u, n) * GT)
            dve.tensor_scalar(pair_of[n], slot_rows[n][:, :, P], 1.0, None, ALU.mult).then_inc(numbers_kept, 1)

        keep_xT(0, 0)

        def unit(u, n):
            if not (isinstance(u, int) and u == U - 1):
                keep_xT(u + 1, (n + 1) % NIN)
            f.lows(dve, u, n % 2)
            keep_numbers(u, n)
            if not early(u, 1):
                keep_y(u - 1, (n - 1) % NIN)

        quads(dve, unit)
        keep_y(U - 1, NIN - 1)


def combine_phase(nc, ctx, x_res, pair_weight, pairs_dram, out):
    def sem(name):
        return ctx.enter_context(nc.semaphore(name))

    CT = 8
    NB = 3
    y = ctx.enter_context(nc.sbuf_tensor("y_pairs", [P, NB, TOP, CT, P], F32))
    loaded = [sem(f"pairs_in{n}") for n in range(NB)]
    first_added, both_added, stored = sem("first_added"), sem("both_added"), sem("stored")
    block = ctx.enter_context(nc.Block())
    steps = NT // CT
    pairs = pairs_dram[0:TOP * NT * P, :].rearrange("(k t p) c -> p k t c", k=TOP, p=P)

    @block.sync
    def _(sp):
        for i in range(steps):
            if i >= NB:
                sp.wait_ge(both_added, i - NB + 1)
            for k in range(TOP):
                sp.dma_start(y[:, i % NB, k], pairs[:, k, i * CT:(i + 1) * CT, :]).then_inc(loaded[i % NB], 16)

    @block.scalar
    def _(act):
        for i in range(steps):
            act.wait_ge(both_added, i + 1)
            act.dma_start(out[i * CT:(i + 1) * CT].rearrange("b t c -> t b c"),
                          x_res[:, i * CT:(i + 1) * CT, :]).then_inc(stored, 16)
        act.wait_ge(stored, 16 * steps)

    @block.vector
    def _(dve):
        for i in range(steps):
            dve.wait_ge(loaded[i % NB], 16 * TOP * (i // NB + 1))
            for k in range(TOP):
                if k:
                    dve.wait_ge(first_added, i + 1)
                for t in range(CT):
                    xt = x_res[:, i * CT + t, :]
                    ins = dve.scalar_tensor_tensor(out=xt, in0=y[:, i % NB, k, t],
                                                   scalar=pair_weight[:, i * CT + t, k:k + 1], in1=xt,
                                                   op0=ALU.mult, op1=ALU.add)
                ins.then_inc(both_added if k else first_added, 1)


def build(nc, d, out):
    xT_dram = nc.dram_tensor("xT_dram", (NG, P, 2, UT), F16).ap()
    slots_dram = nc.dram_tensor("slots_dram", (NU * UT, ROW), U32).ap()
    pairs_dram = nc.dram_tensor("pairs_dram", (TOP * NT * P, P), F32).ap()
    with ExitStack() as whole:
        def sb(name, shape, dt=F32, ctx=whole):
            return ctx.enter_context(nc.sbuf_tensor(name, shape, dt))

        x_res = sb("x_res", [P, NT, P])
        pair_weight = sb("pair_weight", [P, NT, TOP])
        with ExitStack() as mid:
            mask = sb("mask", [P, NT, EA], ctx=mid)
            pair_slot = sb("pair_slot", [P, NT, TOP], U32, ctx=mid)
            unit_expert = sb("unit_expert", [1, NU], I32, ctx=mid)
            x_rows = sb("x_rows", [P, NT, 2 * P], F16, ctx=mid)
            logits = mask[:, :, 0:E]
            with ExitStack() as ctx:
                attention_phase(nc, ctx, d, x_res, x_rows, logits, xT_dram, slots_dram)
            f = Ffn(nc, mid)
            with ExitStack() as ctx:
                router_phase(nc, ctx, d, f, logits, mask, pair_weight, pair_slot, unit_expert)
            f.unit_buffers(nc, mid)
            with ExitStack() as ctx:
                shared_phase(nc, ctx, d, f, x_res, x_rows, mask, pair_slot, xT_dram, slots_dram)
            with ExitStack() as ctx:
                routed_phase(nc, ctx, d, f, x_rows, unit_expert, slots_dram, pairs_dram)
        with ExitStack() as ctx:
            combine_phase(nc, ctx, x_res, pair_weight, pairs_dram, out)


_INS = ["x", "adj"] + ["L0_gnn_" + n for n in ("Wq", "bq", "Wk", "bk", "Wv", "bv", "Wo", "bo")] + \
       ["L0_ffn_" + n for n in ("Wr", "W1s", "b1s", "W2s", "b2s", "W1p", "b1p", "W2p", "b2p")]


def kernel(**inputs):
    import numpy as _np
    import concourse.bacc as _bacc
    from concourse import mybir as _mybir
    from concourse.bass_utils import run_bass_kernel_spmd as _run

    nc = _bacc.Bacc("TRN2", target_bir_lowering=False, num_devices=1)
    arrays = {n: _np.ascontiguousarray(inputs[n]) for n in _INS}
    arrays["ident"] = _np.eye(P, dtype=_np.float32)
    even = (_np.arange(P) % 32 < HD).astype(_np.float32)
    arrays["parity"] = _np.stack([even, 1 - even], 1)
    arrays["before"] = _np.triu(_np.ones((P, P), _np.float32), 1)
    arrays["unit-ids"] = _np.arange(NU, dtype=_np.float32)
    pair = (_np.arange(NT)[None, :, None] * P + _np.arange(P)[:, None, None]
            + _np.arange(TOP)[None, None, :] * NT * P)
    arrays["pair-ids"] = pair.astype(_np.uint32)
    arrays["no_pair"] = _np.full((P, 1), TOP * NT * P, _np.uint32)
    arrays["rank_key"] = (E - _np.arange(E)).astype(_np.float32)
    fed, d = {}, {}
    for name, a in arrays.items():
        fed[f"in_{name}_dram"] = a
        d[name.split("_")[-1] if name in _INS else name] = nc.dram_tensor(
            f"in_{name}_dram", a.shape, _mybir.dt.from_np(a.dtype), kind="ExternalInput").ap()
    out = nc.dram_tensor("out_0_dram", (NT, P, P), _mybir.dt.float32, kind="ExternalOutput").ap()
    build(nc, d, out)
    r = _run(nc, [fed], core_ids=[0])
    return r.results[0]["out_0_dram"]
```
